# Optimizing a Trainium2 kernel written in Bass

```python
import numpy as np
import jax
import jax.numpy as jnp

def _softmax(x, axis=-1):
    return jax.nn.softmax(x, axis=axis)

def _gelu(x):
    return jax.nn.gelu(x, approximate=True)

def _silu(x):
    return jax.nn.silu(x)

def _sigmoid(x):
    return jax.nn.sigmoid(x)

def _layernorm(x, axis=-1, eps=1e-05):
    m = jnp.mean(x, axis=axis, keepdims=True)
    v = jnp.var(x, axis=axis, keepdims=True)
    return (x - m) / jnp.sqrt(v + eps)

def _scatter_add(tgt, idx, src, axis=0):
    return tgt.at[idx].add(src)

def _segment_sum(src, seg, n):
    return jax.ops.segment_sum(src, seg, n)
kernel_name = 'mk_xattn_ffn_d1_seqx_r8_f3c8b1'

def setup_inputs(seed: int=0):
    np.random.seed(seed)
    _w = jnp.asarray

    def _rec_inputs():
        import jax
        import jax.numpy as jnp
        _rk = jax.random.key(seed)
        x = -0.0002928 + 1 * jax.random.normal(jax.random.fold_in(_rk, 1), (64, 64, 256), jnp.float32)
        _lenS = 64 - jax.random.randint(jax.random.fold_in(_rk, 7), (64,), 0, max(1, 64 // 4) + 1, jnp.int32)
        _lenS2 = 64 - jax.random.randint(jax.random.fold_in(_rk, 8), (64,), 0, max(1, 64 // 4) + 1, jnp.int32)
        _ctx_2048P = jax.random.normal(jax.random.fold_in(_rk, 11), (64, 16, 256), jnp.float32)
        _ctx_2048c = jax.random.dirichlet(jax.random.fold_in(_rk, 511), 0.3 * jnp.ones((16,), jnp.float32), (64, 64))
        _ctx_2048t = jnp.einsum('bsk,bkd->bsd', _ctx_2048c, _ctx_2048P)
        _ctx_2048t = _ctx_2048t * jax.lax.rsqrt(jnp.mean(jnp.square(_ctx_2048t)) + 1e-12) * 0.953939
        ctx_2048 = -1.39393e-06 + 0.999914 * (_ctx_2048t + 0.3 * jax.random.normal(jax.random.fold_in(_rk, 611), (64, 64, 256), jnp.float32))
        return (x, ctx_2048)
    x, ctx_2048 = _rec_inputs()

    def _L0_xattn_setup():
        import math
        import jax, jax.numpy as jnp
        import numpy as np
        N_HEADS = 8
        CHANNELS = 64
        K_CH = CHANNELS // N_HEADS
        THETA = 10000.0

        def _rope_freqs(length, dim):
            inv_freq = 1.0 / THETA ** (jnp.arange(0, dim, 2, dtype=jnp.float32) / dim)
            f = jnp.arange(length, dtype=jnp.float32)[:, None] * inv_freq[None, :]
            return jnp.concatenate([f, f], axis=-1)

        def _apply_rotary(pos, t):
            half = t.shape[-1] // 2
            rot = jnp.concatenate([-t[..., half:], t[..., :half]], axis=-1)
            return t * jnp.cos(pos) + rot * jnp.sin(pos)

        def _proj(inp, W, b):
            return jnp.einsum('oc,bct->bot', W, inp) + b[None, :, None]
        key = jax.random.key(seed)
        ks = jax.random.split(key, 10)
        B, C, T = (4, CHANNELS, 256)
        bound = math.sqrt(6.0 / (C + C))

        def w(k):
            return jax.random.uniform(k, (C, C), jnp.float32, -bound, bound)
        return {'x': jax.random.normal(ks[0], (B, C, T), jnp.float32), 'c': jax.random.normal(ks[1], (B, C, T), jnp.float32), 'Wq': w(ks[2]), 'bq': jnp.zeros((C,), jnp.float32), 'Wk': w(ks[3]), 'bk': jnp.zeros((C,), jnp.float32), 'Wv': w(ks[4]), 'bv': jnp.zeros((C,), jnp.float32), 'Wo': w(ks[5]), 'bo': jnp.zeros((C,), jnp.float32)}
    _L0_xattn_all = _L0_xattn_setup()
    _L0_xattn_in = {k: v for k, v in _L0_xattn_all.items() if k in ('Wq', 'bq', 'Wk', 'bk', 'Wv', 'bv', 'Wo', 'bo')}
    del _L0_xattn_all

    def _L0_ffn_setup():
        import jax, jax.numpy as jnp
        import numpy as np
        TOPK = 2
        NORM_TOPK = True
        SCALE = 1.0
        EPS = 1e-09
        key = jax.random.key(seed)
        ks = jax.random.split(key, 9)
        h, i, E = (256, 128, 16)
        std = 0.02
        return {'x': jax.random.normal(ks[0], (1, 256, h), jnp.float32), 'Wr': jax.random.normal(ks[1], (E, h), jnp.float32) * std, 'bias': jnp.zeros((E,), jnp.float32), 'Wg': jax.random.normal(ks[2], (E, h, i), jnp.float32) * std, 'Wu': jax.random.normal(ks[3], (E, h, i), jnp.float32) * std, 'Wd': jax.random.normal(ks[4], (E, i, h), jnp.float32) * std, 'sWg': jax.random.normal(ks[5], (h, i), jnp.float32) * std, 'sWu': jax.random.normal(ks[6], (h, i), jnp.float32) * std, 'sWd': jax.random.normal(ks[7], (i, h), jnp.float32) * std}
    _L0_ffn_all = _L0_ffn_setup()
    _L0_ffn_in = {k: v for k, v in _L0_ffn_all.items() if k in ('Wr', 'bias', 'Wg', 'Wu', 'Wd', 'sWg', 'sWu', 'sWd')}
    del _L0_ffn_all
    return {'x': x, 'ctx_2048': ctx_2048, 'L0_xattn_Wq': _L0_xattn_in['Wq'], 'L0_xattn_bq': _L0_xattn_in['bq'], 'L0_xattn_Wk': _L0_xattn_in['Wk'], 'L0_xattn_bk': _L0_xattn_in['bk'], 'L0_xattn_Wv': _L0_xattn_in['Wv'], 'L0_xattn_bv': _L0_xattn_in['bv'], 'L0_xattn_Wo': _L0_xattn_in['Wo'], 'L0_xattn_bo': _L0_xattn_in['bo'], 'L0_ffn_Wr': _L0_ffn_in['Wr'], 'L0_ffn_bias': _L0_ffn_in['bias'], 'L0_ffn_Wg': _L0_ffn_in['Wg'], 'L0_ffn_Wu': _L0_ffn_in['Wu'], 'L0_ffn_Wd': _L0_ffn_in['Wd'], 'L0_ffn_sWg': _L0_ffn_in['sWg'], 'L0_ffn_sWu': _L0_ffn_in['sWu'], 'L0_ffn_sWd': _L0_ffn_in['sWd']}

def reference(x, ctx_2048, L0_xattn_Wq, L0_xattn_bq, L0_xattn_Wk, L0_xattn_bk, L0_xattn_Wv, L0_xattn_bv, L0_xattn_Wo, L0_xattn_bo, L0_ffn_Wr, L0_ffn_bias, L0_ffn_Wg, L0_ffn_Wu, L0_ffn_Wd, L0_ffn_sWg, L0_ffn_sWu, L0_ffn_sWd):
    import jax
    import jax.numpy as jnp

    def _L0_xattn_ref(x, c, Wq, bq, Wk, bk, Wv, bv, Wo, bo):
        import math
        import jax, jax.numpy as jnp
        import numpy as np
        N_HEADS = 8
        CHANNELS = 64
        K_CH = CHANNELS // N_HEADS
        THETA = 10000.0

        def _rope_freqs(length, dim):
            inv_freq = 1.0 / THETA ** (jnp.arange(0, dim, 2, dtype=jnp.float32) / dim)
            f = jnp.arange(length, dtype=jnp.float32)[:, None] * inv_freq[None, :]
            return jnp.concatenate([f, f], axis=-1)

        def _apply_rotary(pos, t):
            half = t.shape[-1] // 2
            rot = jnp.concatenate([-t[..., half:], t[..., :half]], axis=-1)
            return t * jnp.cos(pos) + rot * jnp.sin(pos)

        def _proj(inp, W, b):
            return jnp.einsum('oc,bct->bot', W, inp) + b[None, :, None]
        b, _, t_t = x.shape
        t_s = c.shape[2]
        q_emb = _rope_freqs(t_t, K_CH)
        k_emb = _rope_freqs(t_s, K_CH)

        def split_heads(t):
            return t.reshape(b, N_HEADS, K_CH, t.shape[2]).transpose(0, 1, 3, 2)
        q = split_heads(_proj(x, Wq, bq))
        k = split_heads(_proj(c, Wk, bk))
        v = split_heads(_proj(c, Wv, bv))
        q = _apply_rotary(q_emb, q)
        k = _apply_rotary(k_emb, k)
        scores = jnp.einsum('bhtc,bhsc->bhts', q, k) / math.sqrt(K_CH)
        p_attn = jax.nn.softmax(scores, axis=-1)
        out = jnp.einsum('bhts,bhsc->bhtc', p_attn, v)
        out = out.transpose(0, 1, 3, 2).reshape(b, N_HEADS * K_CH, t_t)
        return _proj(out, Wo, bo)

    def _L0_ffn_ref(x, Wr, bias, Wg, Wu, Wd, sWg, sWu, sWd):
        import jax, jax.numpy as jnp
        import numpy as np
        TOPK = 2
        NORM_TOPK = True
        SCALE = 1.0
        EPS = 1e-09
        b, s, h = x.shape
        E = Wr.shape[0]
        xt = x.reshape(b * s, h)
        logits = xt @ Wr.T + bias
        probs = jax.nn.softmax(logits, axis=-1)
        topk_val, topk_idx = jax.lax.top_k(probs, TOPK)
        if NORM_TOPK:
            w = topk_val / (jnp.sum(topk_val, axis=-1, keepdims=True) + EPS)
        else:
            w = topk_val
        w = w * SCALE
        g = jnp.einsum('th,ehi->tei', xt, Wg)
        u = jnp.einsum('th,ehi->tei', xt, Wu)
        y = jnp.einsum('tei,eih->teh', jax.nn.silu(g) * u, Wd)
        oh = jax.nn.one_hot(topk_idx, E, dtype=x.dtype)
        routed = jnp.einsum('tke,tk,teh->th', oh, w, y)
        shared = jax.nn.silu(xt @ sWg) * (xt @ sWu) @ sWd
        return (routed + shared).reshape(b, s, h)
    x = x + _L0_xattn_ref(_layernorm(x, axis=-1), ctx_2048, L0_xattn_Wq, L0_xattn_bq, L0_xattn_Wk, L0_xattn_bk, L0_xattn_Wv, L0_xattn_bv, L0_xattn_Wo, L0_xattn_bo)
    x = x + _L0_ffn_ref(_layernorm(x, axis=-1), L0_ffn_Wr, L0_ffn_bias, L0_ffn_Wg, L0_ffn_Wu, L0_ffn_Wd, L0_ffn_sWg, L0_ffn_sWu, L0_ffn_sWd)
    return x

_drawn_inputs = setup_inputs


def setup_inputs(seed=0):
    import zlib

    import numpy as np

    out = dict(_drawn_inputs(seed))
    spreads = {'L0_xattn_bq': (0.0, 0.1),
     'L0_xattn_bk': (0.0, 0.676),
     'L0_xattn_bv': (0.0, 0.389),
     'L0_xattn_bo': (0.0, 0.333),
     'L0_ffn_bias': (0.0, 0.8)}
    factors = {'L0_ffn_Wr': 7.57,
     'L0_ffn_Wg': 7.009,
     'L0_ffn_Wu': 6.93,
     'L0_ffn_Wd': 6.93,
     'L0_ffn_sWg': 5.048,
     'L0_ffn_sWu': 4.928,
     'L0_ffn_sWd': 4.959}
    for name, (base, spread) in spreads.items():
        noise = np.random.default_rng([zlib.crc32(name.encode()), seed]).standard_normal(out[name].shape)
        drawn = base * np.exp(spread * noise) if base else spread * noise
        out[name] = jnp.asarray(drawn.astype(out[name].dtype))
    for name, factor in factors.items():
        out[name] = (out[name] * factor).astype(out[name].dtype)
    return out
```

```python
from contextlib import ExitStack

import concourse.bass as bass
from concourse import mybir

ALU = mybir.AluOpType
ACT = mybir.ActivationFunctionType
AX = mybir.AxisListType
F32 = mybir.dt.float32
BF16 = mybir.dt.bfloat16


class Step:

    def __init__(self, r, i=None, turn=4):
        self.r, self.i, self.turn = r, i, turn

    def batch(self, off=0):
        return self.r + off if self.i is None else self.turn * self.i + (self.r + off)

    def pair(self, off=0):
        h = (self.r + off) // 2
        return h if self.i is None else self.turn // 2 * self.i + h

    def mod(self, n, off=0):
        return (self.r + off) % n

    def odd_pair(self, off=0):
        return (self.r + off) // 2 % 2

    def value(self, per_batch, add):
        v = per_batch * self.r + add
        return v if self.i is None else (self.turn * per_batch) * self.i + v

    def pairs(self, off, per=1, add=0):
        v = per * ((self.r + off) // 2) + add
        return v if self.i is None else (self.turn // 2 * per) * self.i + v

    def turns(self, off, n, per, add=0):
        v = per * ((self.r + off) // n) + add
        return v if self.i is None else (self.turn // n * per) * self.i + v

    def has(self, off, n=64):
        return self.i is not None or 0 <= self.r + off < n


def wait(eng, sem, value, most=None):
    if isinstance(value, int):
        if most is not None:
            value = min(value, most)
        if value <= 0:
            return
    eng.wait_ge(sem, value)


def xattn_moe(nc, x, ctx_in, w6, bias6, rope, ident_in, w_router, b_router, w_gu, w_down, shared_gu, shared_down, counts, below, out):
    NB, C, T = 64, 64, 256
    P = 128
    H, D = 8, 8
    NP = NB // 2
    PARTS = 3
    KR = PARTS * PARTS * D
    MROW = 96
    SCALE = float(D) ** -0.5
    EPS = 1e-5
    E, I = 16, 128
    TT = NP
    NS = 80
    ROW = T + 4
    BIG = 1024.0

    slots = nc.dram_tensor("slots", (NS * P, ROW), F32, kind="Internal").ap()
    results = nc.dram_tensor("results", (2 * TT * P, T), F32, kind="Internal").ap()
    SLOTS = PARTS + 2 * PARTS - 1
    scratch = nc.dram_tensor("parts", (NB, SLOTS, C, T), BF16, kind="Internal").ap()

    with ExitStack() as stack:
        def sb(name, shape, dt=F32):
            return stack.enter_context(nc.sbuf_tensor(name, shape, dt))

        def psum(name):
            return stack.enter_context(nc.psum_tensor(name, [P, 512], F32))

        def sem(name):
            return stack.enter_context(nc.semaphore(name))

        X = sb("X", [P, NP, T])
        ctx_kv = sb("ctx_kv", [P, 4, T])
        ctx_k, ctx_v = ctx_kv[:, 0:2], ctx_kv[:, 2:4]
        w = sb("w", [P, 6, P])
        bias = sb("bias", [P, 6])
        beff = sb("beff", [P, 1])
        tab = sb("tab", [P, 2, T])
        ident = sb("ident", [P, P])
        ident_b = sb("ident_b", [P, P], BF16)
        eps = sb("eps", [P, 1])
        st1 = sb("st1", [P, 2, 6])
        mv1 = sb("mv1", [P, NP, 2])
        std1 = sb("std1", [P, NP])
        rstd1 = sb("rstd1", [P, NP])
        xn = sb("xn", [P, 2, T])
        work = sb("work", [P, 4, 2, T])
        rc, rs, qk, rest = [work[:, i] for i in range(4)]
        parts_sb = sb("parts_sb", [P, 2 * 2 * PARTS * T], BF16)
        parts = parts_sb[:].rearrange("p (n s k t) -> p n s k t", n=2, s=2, k=PARTS)
        QK = sb("QK", [P, 8, H, T], BF16)
        Q = [QK[:, i] for i in range(4)]
        K = [QK[:, 4 + i] for i in range(4)]
        M = sb("M", [P, 2, 2 * H])
        Mb = sb("Mb", [P, 2, 2, 2 * H], BF16)
        Mt = sb("Mt", [4 * H, 2, P], BF16)
        wide = sb("wide", [P, 8 * ROW])
        V = [wide[:, 1024 * i:1024 * i + 1024].rearrange("p (s b h e) -> p s b h e", s=2, b=2, h=H) for i in range(2)]
        Pr = [sb(f"Pr{i}", [P, 2 * T]) for i in range(H)]
        O = sb("O", [P, 2 * T])
        rden = sb("rden", [P, 16])
        On = [sb(f"On{i}", [P, 2, P]) for i in range(2)]
        OT = sb("OT", [P, T])
        st2 = sb("st2", [P, 6])
        mvt = sb("mvt", [P, 2])
        mv2 = sb("mv2", [P, NP, 2])

        XT = QK[:].bitcast(F32).rearrange("p a h t -> p (a h t)").rearrange("p (c n) -> p c n", c=2)
        rows = sb("rows", [P, TT, ROW])
        xs = xn
        xTs = [sb(f"xTs{i}", [P, 2, P]) for i in range(2)]
        wr = sb("wr", [P, 2, E])
        wgu = sb("wgu", [P, E, 2, 2 * I])
        wd = sb("wd", [P, E, T])
        late = parts_sb[:].bitcast(F32)
        sgu = late[:, 0:512].rearrange("p (c i) -> p c i", c=2)
        sd = late[:, 512:768]
        cnt = late[:, 768:1152]
        low = late[:, 1152:1408].rearrange("p (a n) -> p a n", a=2)
        br = sb("br", [P, E])
        std2 = sb("std2", [P, TT])
        rstd2 = sb("rstd2", [P, TT])
        LG, GE, OH0, OH1, MM, PA, PB, PC = [Pr[i] for i in range(8)]
        m1 = sb("m1", [P, 2, TT])
        ix = sb("ix", [P, 2, TT])
        slot_f = sb("slot_f", [P, 2, TT])
        slot = sb("slot", [P, 2, TT], mybir.dt.int32)
        prob = sb("prob", [P, 4, TT])
        gate = sb("gate", [P, 2, TT])
        nt = sb("nt", [P, 4, E])
        owner_f = sb("owner_f", [1, NS])
        owner = sb("owner", [1, NS], mybir.dt.int32)
        blank = sb("blank", [P, ROW])
        xg = wide[:].rearrange("p (a t) -> p a t", a=8)
        sg = work[:, 0:2].rearrange("p a b t -> p a (b t)")
        aT = [work[:, 2 + i].rearrange("p b t -> p (b t)") for i in range(2)]
        ar = [OT[:, P * i:P * i + P] for i in range(2)]
        pair_in = XT.rearrange("p c n -> p (c n)")[:, 0:16 * T].rearrange("p (m k n t) -> p m k n t", m=2, k=2, n=4)
        half_sum = [Pr[4 + n // 2][:, T * (n % 2):T * (n % 2) + T] for n in range(4)]
        ys = ctx_kv

        bank_s = [psum(f"bank_s{i}") for i in range(2)]
        bank_st = [psum(f"bank_st{i}") for i in range(2)]
        bank_o = [psum(f"bank_o{i}") for i in range(2)]
        bank_a = psum("bank_a")
        bank_b = psum("bank_b")
        tile_bank, logit_bank = (bank_a, bank_b), bank_s
        g_bank, u_bank = bank_st, bank_o
        y_bank = (bank_s, (bank_a, bank_b))
        before_bank, all_bank = bank_a, bank_b
        up_bank, mid_bank, down_bank = bank_st, bank_o, bank_s

        s_x = [sem(f"s_xin{g}") for g in range(8)]
        s_w = sem("s_w")
        s_zero = sem("s_zero")
        s_wd = sem("s_wd")
        s_ck = [sem(f"s_ck{i}") for i in range(2)]
        s_cv = [sem(f"s_cv{i}") for i in range(2)]
        s_ptw = [sem(f"s_ptw{i}") for i in range(2)]
        s_stk = [sem(f"s_stk{i}") for i in range(4)]
        s_mr = [sem(f"s_mr{i}") for i in range(2)]
        s_st1 = sem("s_st1")
        s_mv1 = sem("s_mv1")
        s_std1 = sem("s_std1")
        s_rstd1 = sem("s_rstd1")
        s_xn = sem("s_xn")
        s_qp = sem("s_qp")
        s_kp = sem("s_kp")
        s_vp = sem("s_vp")
        s_rq = sem("s_rq")
        s_rk = sem("s_rk")
        s_qk = sem("s_qk")
        s_p1 = sem("s_p1")
        s_r1 = sem("s_r1")
        s_p2 = sem("s_p2")
        s_pt = sem("s_pt")
        s_S = sem("s_S")
        s_red = sem("s_red")
        s_hi = sem("s_hi")
        s_msp = sem("s_msp")
        s_TM = sem("s_TM")
        s_tme = sem("s_tme")
        s_ST = sem("s_ST")
        s_exp = sem("s_exp")
        s_PV = sem("s_PV")
        s_Ve = sem("s_Ve")
        s_Oe = sem("s_Oe")
        s_T1 = sem("s_T1")
        s_rc = sem("s_rc")
        s_On = sem("s_On")
        s_BT = sem("s_BT")
        s_BTe = sem("s_BTe")
        s_WO = sem("s_WO")
        s_x2 = sem("s_x2")
        s_st2 = sem("s_st2")
        s_mvt = sem("s_mvt")
        s_mv2 = sem("s_mv2")
        s_bo = sem("s_bo")
        s_beff = sem("s_beff")
        s_wx = sem("s_wx")
        s_blank = sem("s_blank")
        s_fill = sem("s_fill")
        s_std2 = sem("s_std2")
        s_rstd2 = sem("s_rstd2")
        s_id = sem("s_id")
        s_xs = sem("s_xs")
        s_xcp = sem("s_xcp")
        s_xt = sem("s_xt")
        s_xte = sem("s_xte")
        s_xts = sem("s_xts")
        s_lg = sem("s_lg")
        s_lge = sem("s_lge")
        s_mm = sem("s_mm")
        s_pos = sem("s_pos")
        s_ex = sem("s_ex")
        s_rt = sem("s_rt")
        s_slot = sem("s_slot")
        s_sc0 = sem("s_sc0")
        s_id1 = sem("s_id1")
        s_owner = sem("s_owner")
        s_gu = sem("s_gu")
        s_sil = sem("s_sil")
        s_act = sem("s_act")
        s_dn = sem("s_dn")
        s_sh = sem("s_sh")
        s_t = sem("s_t")
        s_te = sem("s_te")
        s_g = sem("s_g")
        s_si = sem("s_si")
        s_a = sem("s_a")
        s_h = sem("s_h")
        s_he = sem("s_he")
        s_d = sem("s_d")
        s_ye = sem("s_ye")
        s_comb = sem("s_comb")
        s_hs = sem("s_hs")
        s_sc1 = sem("s_sc1")
        s_xg = [sem(f"s_xg{i}") for i in range(8)]
        s_put = [sem(f"s_put{i}") for i in range(4)]
        s_y = [sem(f"s_y{i}") for i in range(2)]
        s_o = [sem(f"s_o{i}") for i in range(2)]

        FIRST, LAST = -8, 66
        LOOP = (4, 56)

        def steps(eng, step, first=FIRST, loop=LOOP, last=LAST, turn=4):
            for b in range(first, loop[0]):
                step(Step(b, None, turn))
            with eng.Fori(loop[0] // turn, loop[1] // turn) as i:
                for r in range(turn):
                    step(Step(r, i, turn))
            for b in range(loop[1], last):
                step(Step(b, None, turn))

        def apart(eng):
            eng.wait_ge(s_w, 48)

        block = stack.enter_context(nc.Block())

        @block.sync
        def _(sp):
            for g in range(2):
                sp.dma_start(X[:, 4 * g:4 * g + 4, :],
                             x.rearrange("(n p) t -> p n t", p=P)[:, 4 * g:4 * g + 4, :]).then_inc(s_x[g], 16)
            sp.dma_start(bias[:], bias6).then_inc(s_w, 16)
            sp.dma_start(tab[:], rope).then_inc(s_w, 16)
            sp.dma_start(ident[:], ident_in).then_inc(s_w, 16)
            sp.wait_ge(s_zero, 1)
            sp.dma_start(w[0:C, :, 0:C], w6).then_inc(s_wd, 16)
            sp.dma_start(w[C:P, :, C:P], w6).then_inc(s_wd, 16)
            for g in range(2, 8):
                sp.dma_start(X[:, 4 * g:4 * g + 4, :],
                             x.rearrange("(n p) t -> p n t", p=P)[:, 4 * g:4 * g + 4, :]).then_inc(s_x[g], 16)
            sp.wait_ge(s_zero, 13)

            def alone(sem_, value):
                wait(sp, sem_, known(value))

            def known(index):
                if not isinstance(index, int):
                    sp.compute_val(index)
                return index

            def load(dst, sems, at, off, pair):
                p = at.odd_pair(off)
                sp.dma_start(dst[:, p:p + 1, :].rearrange("p a t -> p (a t)"),
                             ctx_in.rearrange("(n p) t -> n p t", p=P)[bass.ds(pair, 1), :, :]
                             .rearrange("n p t -> (n p) t")).then_inc(sems[p], 16)

            def weights(n):
                e = 4 * n
                for c in range(2):
                    sp.dma_start(wgu[:, e:e + 4, c, :],
                                 w_gu.rearrange("e (c p) i -> p e c i", p=P)[:, e:e + 4, c, :]).then_inc(s_wx, 16)
                sp.dma_start(wd[:, e:e + 4, :], w_down[e:e + 4].rearrange("e p t -> p e t")).then_inc(s_wx, 16)
                if n == 0:
                    sp.dma_start(wr[:], w_router.rearrange("(c p) i -> p c i", p=P)).then_inc(s_wx, 16)
                    sp.dma_start(br[:], b_router).then_inc(s_wx, 16)

            def late_weights():
                for p in range(2):
                    sp.wait_ge(s_ptw[p], 64 * NP // 2)
                sp.dma_start(sgu, shared_gu.rearrange("(c p) i -> p c i", p=P)).then_inc(s_wx, 16)
                for dst, src in ((sd, shared_down), (cnt, counts), (low, below)):
                    sp.dma_start(dst, src).then_inc(s_wx, 16)

            def fill(n):
                alone(s_blank, 2)
                sp.dma_start(slots.rearrange("(n p) t -> p n t", p=P)[:, 10 * n:10 * n + 10, :],
                             blank[:].rearrange("p (o t) -> p o t", o=1).to_broadcast([P, 10, ROW])).then_inc(s_fill, 16)

            def step(at):
                if at.i is None and 0 <= at.r < 4:
                    weights(at.r)
                if at.i is None and 56 <= at.r < 64:
                    fill(at.r - 56)
                if at.i is None and at.r == 62:
                    late_weights()
                if at.r % 2 == 0 and at.has(8):
                    pair = known(at.pair(8))
                    alone(s_kp, at.pairs(8, add=-1))
                    load(ctx_k, s_ck, at, 8, pair)
                if at.r % 2 == 0 and at.has(4):
                    pair = known(at.pair(4))
                    alone(s_vp, at.pairs(4, add=-1))
                    load(ctx_v, s_cv, at, 4, pair)
                if at.has(3):
                    batch = known(at.batch(3))
                    c = at.mod(4, 3)
                    written, used = known(at.turns(3, 4, 64, 64)), known(at.value(8, 0))
                    alone(s_ptw[at.odd_pair(3)], written)
                    alone(s_ST, used)
                    src = scratch[bass.ds(batch, 1)].rearrange("a s c t -> (a s) (c t)")
                    for dst, slot, turn in ((Q[c], 0, 0), (K[c], PARTS, C * T)):
                        g = src[slot:slot + 1]
                        rows = [[turn, PARTS], [H * T, PARTS * D], [1, H * T]]
                        sp.dma_start(dst[0:KR].rearrange("r h t -> r (h t)"),
                                     bass.AP(tensor=g.tensor, offset=g.offset, ap=rows)).then_inc(s_stk[c], 16)
                if at.has(1):
                    alone(s_tme, at.value(1, 2))
                    c = at.mod(4, 1)
                    m = at.mod(2, 1)
                    sp.dma_start(Q[c][MROW:MROW + 2].rearrange("r h t -> r (h t)"), Mt[:, m, :]).then_inc(s_mr[m], 16)
                if at.r % 2 == 1 and at.has(5):
                    pair = known(at.pair(5))
                    alone(s_pt, at.pairs(5, add=1))
                    p = at.odd_pair(5)
                    dst = scratch.rearrange("(n b) s c t -> n b c s t", b=2)
                    for half in range(2):
                        to = dst[bass.ds(pair, 1), half:half + 1].rearrange("n b c s t -> (n b c) s t")
                        own = parts[C * half:C * half + C, p]
                        sp.dma_start(to[:, 0:2 * PARTS], own.rearrange("p s k t -> p (s k) t")).then_inc(s_ptw[p], 16)
                        sp.dma_start(to[:, 2 * PARTS:SLOTS], own[:, 1, 0:PARTS - 1, :]).then_inc(s_ptw[p], 16)

            steps(sp, step)

            def feed(at):
                if at.has(0, NS):
                    tile, read, sent = known(at.batch()), known(at.value(1, -7)), known(at.turns(-8, 4, 16, 16))
                    alone(s_t, read)
                    alone(s_put[at.mod(4)], sent)
                    sp.dma_start(xg[:, at.mod(8), :],
                                 slots.rearrange("(n p) t -> n p t", p=P)[bass.ds(tile, 1)]
                                 .rearrange("n p t -> (n p) t")).then_inc(s_xg[at.mod(8)], 16)

            sp.wait_ge(s_sc0, 16 * TT)
            sp.wait_ge(s_sc1, 16 * TT)
            sp.wait_ge(s_owner, 1)
            steps(sp, feed, 0, (8, 72), NS, 8)

            for i in range(4):
                sp.wait_ge(s_put[i], 16 * (NS // 4))
            res = results[0:2 * TT * P].rearrange("(k g n p) t -> p g k n t", k=2, n=4, p=P)

            def gather(at):
                if at.has(0, TT // 4):
                    g, m = known(at.batch()), at.mod(2)
                    used = known(at.value(1, -1))
                    alone(s_comb, used)
                    for k in range(2):
                        sp.dma_start(pair_in[:, m, k], res[:, bass.ds(g, 1), k].rearrange("p g n t -> p (g n) t")).then_inc(s_y[m], 16)
                if at.has(-1, TT // 4):
                    g, m = known(at.batch(-1)), at.mod(2, -1)
                    made = known(at.value(1, 0))
                    alone(s_comb, made)
                    sp.dma_start(out.rearrange("(g n p) t -> p g n t", n=4, p=P)[:, bass.ds(g, 1)].rearrange("p g n t -> p (g n) t"),
                                 X[:, bass.ds(4 * g, 4), :]).then_inc(s_o[m], 16)

            steps(sp, gather, 0, (2, 8), 9, 2)
            for i in range(2):
                sp.wait_ge(s_o[i], 16 * 4)

        @block.gpsimd
        def _(pool):
            pieces = [(w[:], 0.0)]
            for i in range(4):
                pieces += [(Q[i][64:P], 0.0), (K[i][64:MROW], 0.0), (K[i][MROW:P], -1.0)]
            for i in range(2):
                pieces += [(V[i][:, :, :, :, 0:8], 0.0), (V[i][:, :, :, :, 9:32], 0.0), (V[i][:, :, :, :, 8:9], 1.0)]
            nc.gpsimd.memset(blank[:], 0.0).then_inc(s_blank, 1)
            pool.wait_ge(s_blank, 1)
            nc.gpsimd.iota(blank[:, T:T + 1].bitcast(mybir.dt.int32), pattern=[[0, 1]], base=2 * TT * P,
                           channel_multiplier=1).then_inc(s_blank, 1)
            pool.wait_ge(s_blank, 2)
            for n, (piece, fill) in enumerate(pieces):
                wait(pool, s_zero, n)
                nc.gpsimd.memset(piece, fill).then_inc(s_zero, 1)

            def step(at):
                if at.r % 2 == 0 and at.has(6):
                    p = at.odd_pair(6)
                    wait(pool, s_rq, at.pairs(6, add=1))
                    wait(pool, s_rk, at.pairs(6, add=1))
                    wait(pool, s_pt, at.pairs(6))
                    nc.gpsimd.tensor_tensor(qk[:], rc[:], rs[:], ALU.add).then_inc(s_qk, 1)
                    v = 64 * (((at.r + 6) // 2) // 2)
                    wait(pool, s_ptw[p], v if at.i is None else 64 * at.i + v)
                    nc.gpsimd.tensor_tensor(parts[:, p, :, 0, :], rc[:], rs[:], ALU.add).then_inc(s_p1, 1)
                    wait(pool, s_p1, at.pairs(6, add=1))
                    nc.gpsimd.tensor_tensor(rest[:], qk[:], parts[:, p, :, 0, :], ALU.subtract).then_inc(s_r1, 1)
                    nc.gpsimd.tensor_tensor(parts[:, p, :, 1, :], qk[:], parts[:, p, :, 0, :],
                                            ALU.subtract).then_inc(s_p2, 1)
                    wait(pool, s_p2, at.pairs(6, add=1))
                    nc.gpsimd.tensor_tensor(parts[:, p, :, 2, :], rest[:], parts[:, p, :, 1, :],
                                            ALU.subtract).then_inc(s_pt, 1)

            steps(pool, step)

            ids = rows[:, :, T:T + 1].bitcast(mybir.dt.int32)
            nc.gpsimd.iota(ids, pattern=[[P, TT], [0, 1]], base=0, channel_multiplier=1).then_inc(s_id, 1)
            nc.gpsimd.memset(rows[:, :, T + 1:ROW], 0.0).then_inc(s_id, 1)

            pool.wait_ge(s_slot, 1)
            pool.wait_ge(s_id, 2)
            pool.wait_ge(s_fill, 16 * 8)
            for k in range(2):
                if k == 1:
                    pool.wait_ge(s_id1, 1)
                for n in range(TT):
                    pool.indirect_dma_start(
                        out=slots, out_offset=bass.IndirectOffsetOnAxis(ap=slot[:, k, n:n + 1], axis=0),
                        in_=rows[:, n, :], in_offset=None).then_inc((s_sc0, s_sc1)[k], 16)

            def put(at):
                if at.has(-3, NS):
                    if at.i is not None:
                        pool.compute_val(at.value(1, -2))
                    apart(pool)
                    wait(pool, s_ye, at.value(1, -2))
                    pool.indirect_dma_start(
                        out=results, out_offset=bass.IndirectOffsetOnAxis(
                            ap=xg[:, at.mod(8, -3), T:T + 1].bitcast(mybir.dt.int32), axis=0),
                        in_=ys[:, at.mod(4, -3), :], in_offset=None,
                        bounds_check=2 * TT * P - 1, oob_is_err=False).then_inc(s_put[at.mod(4, -3)], 16)

            steps(pool, put, 0, (8, 80), NS + 3, 8)

        @block.scalar
        def _(act):
            act.wait_ge(s_mv1, 4)
            act.wait_ge(s_w, 48)
            act.wait_ge(s_beff, 1)
            nc.scalar.activation(std1[:, 0:4], mv1[:, 0:4, 1], ACT.Sqrt, bias=eps[:, 0:1]).then_inc(s_std1, 1)
            act.wait_ge(s_mv1, NP)
            nc.scalar.activation(std1[:, 4:NP], mv1[:, 4:NP, 1], ACT.Sqrt, bias=eps[:, 0:1]).then_inc(s_std1, 1)

            def step(at):
                for k in range(H):
                    if at.has(0):
                        wait(act, s_ST, at.value(8, k + 1))
                        if k % 4 == 0:
                            wait(act, s_PV, at.value(2, -1 + k // 4))
                        nc.scalar.activation(Pr[k][:], bank_st[k % 2][:], ACT.Exp, scale=SCALE).then_inc(s_exp, 1)
                    if k == 2 and at.has(-1):
                        wait(act, s_PV, at.value(2, 0))
                        wait(act, s_T1, at.value(1, -1))
                        nc.scalar.activation(O[:], bank_o[at.mod(2, -1)][:], ACT.Copy).then_inc(s_Oe, 1)
                    if k == 5 and at.r % 2 == 0 and at.has(2):
                        wait(act, s_vp, at.pairs(2, add=1))
                        wait(act, s_PV, at.pairs(2, 4, -4))
                        nc.scalar.activation(
                            V[at.odd_pair(2)][:].rearrange("p s b h e -> p (s b h) e")[:, :, 0:D],
                            bank_a[:].rearrange("p (g e) -> p g e", e=D)[:, 0:32, :], ACT.Copy).then_inc(s_Ve, 1)
                    if k == 6 and at.r % 2 == 0 and at.has(-2):
                        wait(act, s_BT, at.pairs(-2, add=1))
                        wait(act, s_WO, at.pairs(-2))
                        nc.scalar.activation(OT[:], bank_b[:, 0:T], ACT.Copy).then_inc(s_BTe, 1)

            steps(act, step)

            act.wait_ge(s_mv2, NP)
            nc.scalar.activation(std2[:], mv2[:, :, 1], ACT.Sqrt, bias=eps[:, 0:1]).then_inc(s_std2, 1)

            def copies(at):
                if at.has(0, TT):
                    wait(act, s_xs, at.value(1, 1))
                    apart(act)
                    nc.scalar.activation(rows[:, bass.ds(at.batch(), 1), 0:T].rearrange("p a t -> p (a t)"),
                                         xs[:, at.mod(2), :], ACT.Copy).then_inc(s_xcp, 1)
                    wait(act, s_xt, at.value(1, 1))
                    apart(act)
                    nc.scalar.activation(XT[:, :, bass.ds(P * at.batch(), P)],
                                         tile_bank[at.mod(2)][:, 0:2 * P].rearrange("p (c n) -> p c n", c=2),
                                         ACT.Copy).then_inc(s_xte, 1)

            steps(act, copies, 0, (2, 32), TT, 2)

            act.wait_ge(s_ex, 1)
            nc.scalar.activation(PC[:], PB[:], ACT.Exp).then_inc(s_ex, 1)
            nc.scalar.activation(prob[:, 0, :], prob[:, 1, :], ACT.Exp).then_inc(s_ex, 1)

            def shared_silu(at):
                if at.has(0, 8):
                    wait(act, s_gu, at.value(1, 1))
                    wait(act, s_act, at.value(1, -1))
                    nc.scalar.activation(sg[:, at.mod(2), :], g_bank[at.mod(2)][:], ACT.Silu).then_inc(s_sil, 1)

            steps(act, shared_silu, 0, (2, 8), 8, 2)

            def slot_tile(at):
                if at.has(0, NS):
                    wait(act, s_t, at.value(1, 1))
                    wait(act, s_g, at.value(1, -1))
                    nc.scalar.activation(xTs[at.mod(2)][:], tile_bank[at.mod(2)][:, 0:2 * P]
                                         .rearrange("p (c n) -> p c n", c=2), ACT.Copy).then_inc(s_te, 1)
                if at.has(-1, NS):
                    wait(act, s_g, at.value(1, 0))
                    wait(act, s_a, at.value(1, -2))
                    nc.scalar.activation(sg[:, at.mod(2, -1), 0:I], up_bank[at.mod(2, -1)][:, 0:I],
                                         ACT.Silu).then_inc(s_si, 1)
                if at.has(-2, NS):
                    wait(act, s_h, at.value(1, -1))
                    wait(act, s_d, at.value(1, -3))
                    nc.scalar.activation(aT[at.mod(2, -2)][:, 0:P], mid_bank[at.mod(2, -2)][:, 0:P],
                                         ACT.Copy).then_inc(s_he, 1)

            act.wait_ge(s_dn, 8)
            act.wait_ge(s_lge, TT)
            act.wait_ge(s_act, 8)
            steps(act, slot_tile, 0, (8, 80), NS + 2, 8)

        @block.vector
        def _(dve):
            nc.vector.memset(eps[:], EPS)
            dve.wait_ge(s_w, 48)
            nc.vector.tensor_copy(ident_b[:], ident[:]).then_inc(s_bo, 1)
            dve.wait_ge(s_bo, 2)
            nc.vector.tensor_tensor(beff[:], bank_a[:, 0:1], bias[:, 4:5], ALU.add).then_inc(s_beff, 1)

            def stats(p):
                if p >= 2:
                    dve.wait_ge(s_mv1, p - 1)
                nc.vector.bn_stats(st1[:, p % 2, :], X[:, p, :]).then_inc(s_st1, 1)
                dve.wait_ge(s_st1, p + 1)
                nc.vector.bn_aggr(mv1[:, p, :], st1[:, p % 2, :]).then_inc(s_mv1, 1)

            dve.wait_ge(s_x[0], 16)
            for p in range(4):
                stats(p)
            dve.wait_ge(s_std1, 1)
            nc.vector.reciprocal(rstd1[:, 0:4], std1[:, 0:4]).then_inc(s_rstd1, 1)

            def rest_of_stats():
                for p in range(4, NP):
                    if p % 4 == 0:
                        dve.wait_ge(s_x[p // 4], 16)
                    stats(p)
                dve.wait_ge(s_std1, 2)
                nc.vector.reciprocal(rstd1[:, 4:NP], std1[:, 4:NP]).then_inc(s_rstd1, 1)

            def products(bank, col, half, done, projected, at):
                wait(dve, projected, at.pairs(6, add=1))
                wait(dve, s_p1, at.pairs(6))
                nc.vector.scalar_tensor_tensor(rc[:, half, :], bank[:, 0:T], bias[:, col:col + 1],
                                               tab[:, 0, :], ALU.add, ALU.mult)
                nc.vector.scalar_tensor_tensor(rs[:, half, :], bank[:, T:2 * T], bias[:, col + 1:col + 2],
                                               tab[:, 1, :], ALU.add, ALU.mult).then_inc(done, 1)

            def step(at):
                if at.has(1):
                    c = at.mod(2, 1)
                    wait(dve, s_red, at.value(8, 16))
                    wait(dve, s_TM, at.value(1, 0))
                    nc.vector.tensor_copy(Mb[:, c, 0, :], M[:, c, :]).then_inc(s_hi, 1)
                    wait(dve, s_hi, at.value(1, 2))
                    nc.vector.tensor_tensor(Mb[:, c, 1, :], M[:, c, :], Mb[:, c, 0, :], ALU.subtract).then_inc(s_msp, 1)
                for k in range(H):
                    if at.r % 2 == 1 and at.has(-3):
                        if k == 2:
                            wait(dve, s_x2, at.pairs(-3, add=1))
                            wait(dve, s_mvt, at.pairs(-3))
                        if k == 3:
                            wait(dve, s_st2, at.pairs(-3, add=1))
                        if k == 4:
                            wait(dve, s_mvt, at.pairs(-3, add=1))
                    if at.has(2):
                        c = at.mod(2)
                        wait(dve, s_S, at.value(8, 16 + k + 1))
                        if k == 0:
                            wait(dve, s_msp, at.value(1, 1))
                        nc.vector.tensor_reduce(M[:, c, 2 * k:2 * k + 2],
                                                bank_s[k % 2][:].rearrange("p (a s) -> p a s", a=2),
                                                AX.X, ALU.max).then_inc(s_red, 1)
                    if k == 0 and at.r % 2 == 0 and at.has(6):
                        p = at.odd_pair(6)
                        pair = at.pair(6)
                        dve.wait_ge(s_rstd1, 1 if at.i is None and pair < 4 else 2)
                        wait(dve, s_qp, at.pairs(6, add=-1))
                        nc.vector.tensor_scalar(
                            xn[:, p, :], X[:, bass.ds(pair, 1), :].rearrange("p a t -> p (a t)"),
                            mv1[:, bass.ds(pair, 1), 0:1].rearrange("p a t -> p (a t)"),
                            rstd1[:, bass.ds(pair, 1)], ALU.subtract, ALU.mult).then_inc(s_xn, 1)
                    if k == 0 and at.r % 2 == 1 and at.has(-3):
                        pair = at.pair(-3)
                        xp = X[:, bass.ds(pair, 1), :].rearrange("p a t -> p (a t)")
                        wait(dve, s_WO, at.pairs(-3, add=1))
                        nc.vector.scalar_tensor_tensor(xp, bank_a[:, 0:T], beff[:, 0:1], xp,
                                                       ALU.add, ALU.add).then_inc(s_x2, 1)
                    if k == 2 and at.r % 2 == 1 and at.has(-3):
                        nc.vector.bn_stats(st2[:], X[:, bass.ds(at.pair(-3), 1), :]
                                           .rearrange("p a t -> p (a t)")).then_inc(s_st2, 1)
                    if k == 3 and at.r % 2 == 1 and at.has(-3):
                        nc.vector.bn_aggr(mvt[:], st2[:]).then_inc(s_mvt, 1)
                    if k == 4 and at.r % 2 == 1 and at.has(-3):
                        nc.vector.tensor_copy(mv2[:, bass.ds(at.pair(-3), 1), :]
                                              .rearrange("p a t -> p (a t)"), mvt[:]).then_inc(s_mv2, 1)
                    if k == 1 and at.has(1):
                        m = at.mod(2, 1)
                        bank = (bank_b if at.r % 2 else bank_a)[:].bitcast(BF16)
                        wait(dve, s_TM, at.value(1, 2))
                        v = 16 * ((at.r + 1) // 2)
                        wait(dve, s_mr[m], v if at.i is None else 32 * at.i + v)
                        nc.vector.tensor_copy(Mt[:, m, :], bank[0:4 * H, 0:P]).then_inc(s_tme, 1)
                    if k == 3 and at.r % 2 == 0 and at.has(6):
                        products(bank_b, 0, 0, s_rq, s_qp, at)
                    if k == 4 and at.r % 2 == 0 and at.has(6):
                        products(bank_a, 2, 1, s_rk, s_kp, at)
                    if k == 5 and at.has(-1):
                        o = bank_b[:].rearrange("p (g e) -> p g e", e=32)
                        wait(dve, s_T1, at.value(1, 0))
                        wait(dve, s_On, at.value(1, -1))
                        nc.vector.reciprocal(rden[:], o[:, :, D]).then_inc(s_rc, 1)
                        wait(dve, s_rc, at.value(1, 0))
                        half = at.mod(2, -1)
                        if half == 0:
                            wait(dve, s_BT, at.pairs(-1, add=-1))
                        nc.vector.tensor_tensor(
                            On[at.odd_pair(-1)][:, :, C * half:C * half + C].rearrange("p a (h e) -> p a h e", e=D),
                            o[:, :, 0:D].rearrange("p (a h) e -> p a h e", a=2),
                            rden[:].rearrange("p (a h o) -> p a h o", a=2, o=1).to_broadcast([P, 2, H, D]),
                            ALU.mult).then_inc(s_On, 1)
                if at.i is None and at.r == -8:
                    pass
                if at.i is None and at.r == -4:
                    rest_of_stats()

            steps(dve, step)

            dve.wait_ge(s_std2, 1)
            nc.vector.reciprocal(rstd2[:], std2[:]).then_inc(s_rstd2, 1)
            dve.wait_ge(s_rstd2, 1)
            dve.wait_ge(s_mv2, NP)
            dve.wait_ge(s_wx, 16 * 18)

            def tokens(at):
                if at.has(0, TT):
                    n = at.batch()
                    wait(dve, s_xt, at.value(1, -1))
                    wait(dve, s_xcp, at.value(1, -1))
                    apart(dve)
                    nc.vector.tensor_scalar(
                        xs[:, at.mod(2), :], X[:, bass.ds(n, 1), :].rearrange("p a t -> p (a t)"),
                        mv2[:, bass.ds(n, 1), 0:1].rearrange("p a t -> p (a t)"), rstd2[:, bass.ds(n, 1)],
                        ALU.subtract, ALU.mult).then_inc(s_xs, 1)
                if at.has(-1, TT):
                    wait(dve, s_xte, at.value(1, 0))
                    wait(dve, s_lg, at.value(1, -2))
                    nc.vector.tensor_copy(xTs[at.mod(2, -1)][:], tile_bank[at.mod(2, -1)][:, 0:2 * P]
                                          .rearrange("p (c n) -> p c n", c=2)).then_inc(s_xts, 1)
                if at.has(-2, TT):
                    wait(dve, s_lg, at.value(1, -1))
                    apart(dve)
                    nc.vector.tensor_tensor(LG[:, bass.ds(E * at.batch(-2), E)], logit_bank[at.mod(2, -2)][:, 0:E],
                                            br[:], ALU.add).then_inc(s_lge, 1)

            steps(dve, tokens, 0, (4, 32), TT + 2, 2)

            done = [0]

            def then(ins):
                done[0] += 1
                ins.then_inc(s_rt, 1)
                dve.wait_ge(s_rt, done[0])

            def by_expert(t):
                return t[:].rearrange("p (n e) -> p n e", e=E)

            def over_experts(v):
                return v.rearrange("p (n o) -> p n o", o=1).to_broadcast([P, TT, E])

            def over_tiles(v):
                return v.rearrange("p (o e) -> p o e", o=1).to_broadcast([P, TT, E])

            dve.wait_ge(s_lge, TT)
            number = over_tiles(cnt[:, 0:E])
            for k, oh in enumerate((OH0, OH1)):
                logits = LG if k == 0 else PA
                then(nc.vector.tensor_reduce(m1[:, k, :], by_expert(logits), AX.X, ALU.max))
                then(nc.vector.tensor_tensor(by_expert(GE), by_expert(logits), over_experts(m1[:, k, :]), ALU.is_ge))
                then(nc.vector.tensor_tensor(by_expert(PB), by_expert(GE), number, ALU.mult))
                then(nc.vector.tensor_reduce(ix[:, k, :], by_expert(PB), AX.X, ALU.min))
                then(nc.vector.tensor_tensor(by_expert(oh), number, over_experts(ix[:, k, :]), ALU.is_equal))
                if k == 0:
                    then(nc.vector.scalar_tensor_tensor(PA[:], OH0[:], -3e38, LG[:], ALU.mult, ALU.add))
            nc.vector.tensor_tensor(MM[:], OH0[:], OH1[:], ALU.add).then_inc(s_mm, 1)
            nc.vector.tensor_tensor(prob[:, 1, :], m1[:, 1, :], m1[:, 0, :], ALU.subtract)
            nc.vector.tensor_tensor(by_expert(PB), by_expert(LG), over_experts(m1[:, 0, :]), ALU.subtract).then_inc(s_ex, 1)
            dve.wait_ge(s_pos, 1)
            then(nc.vector.memset(PA[:, 0:E], 0.0))
            then(nc.vector.tensor_copy(PA[:, E:TT * E], all_bank[:, 0:(TT - 1) * E]))
            a, b = PA, GE
            for d in (1, 2, 4, 8, 16):
                nc.vector.tensor_copy(b[:, 0:d * E], a[:, 0:d * E])
                then(nc.vector.tensor_tensor(b[:, d * E:], a[:, d * E:], a[:, 0:(TT - d) * E], ALU.add))
                a, b = b, a
            then(nc.vector.tensor_tensor(nt[:, 0, :], a[:, (TT - 1) * E:], all_bank[:, (TT - 1) * E:TT * E], ALU.add))
            then(nc.vector.tensor_tensor(b[:].rearrange("p (e n) -> p e n", e=E),
                                         nt[:, 0, :].rearrange("p (e o) -> p e o", o=1).to_broadcast([P, E, TT]),
                                         cnt[:, E:E + TT].rearrange("p (o n) -> p o n", o=1).to_broadcast([P, E, TT]),
                                         ALU.is_gt))
            then(nc.vector.tensor_reduce(nt[:, 1, :], b[:].rearrange("p (e n) -> p e n", e=E), AX.X, ALU.add))
            upto = cnt[:, E + TT + NS:].rearrange("p (e f) -> p e f", e=E)
            then(nc.vector.tensor_tensor(b[:, 0:E * E].rearrange("p (e f) -> p e f", e=E), upto,
                                         nt[:, 1, :].rearrange("p (o f) -> p o f", o=1).to_broadcast([P, E, E]), ALU.mult))
            then(nc.vector.tensor_reduce(nt[:, 2, :], b[:, 0:E * E].rearrange("p (e f) -> p e f", e=E), AX.X, ALU.add))
            then(nc.vector.tensor_tensor(nt[:, 3, :], nt[:, 2, :], nt[:, 1, :], ALU.subtract))
            then(nc.vector.tensor_tensor(a[:], a[:], before_bank[:], ALU.add))
            then(nc.vector.tensor_scalar(nt[:, 3, :], nt[:, 3, :], float(P), None, ALU.mult))
            then(nc.vector.tensor_tensor(by_expert(a), by_expert(a), over_tiles(nt[:, 3, :]), ALU.add))
            for k, oh in enumerate((OH0, OH1)):
                then(nc.vector.tensor_tensor(b[:], a[:], oh[:], ALU.mult))
                then(nc.vector.tensor_reduce(slot_f[:, k, :], by_expert(b), AX.X, ALU.add))
            nc.vector.tensor_copy(slot[:], slot_f[:]).then_inc(s_slot, 1)
            big = xg[0:1].rearrange("p a t -> p (a t)")[:, 0:NS * E].rearrange("p (j e) -> p j e", e=E)
            then(nc.vector.tensor_tensor(big, nt[0:1, 2, :].rearrange("p (o e) -> p o e", o=1).to_broadcast([1, NS, E]),
                                         cnt[0:1, E + TT:E + TT + NS].rearrange("p (j o) -> p j o", o=1)
                                         .to_broadcast([1, NS, E]), ALU.is_le))
            then(nc.vector.tensor_reduce(owner_f[:], big, AX.X, ALU.add))
            then(nc.vector.tensor_scalar(owner_f[:], owner_f[:], float(E - 1), None, ALU.min))
            nc.vector.tensor_copy(owner[:], owner_f[:]).then_inc(s_owner, 1)
            dve.wait_ge(s_ex, 3)
            then(nc.vector.tensor_reduce(prob[:, 2, :], by_expert(PC), AX.X, ALU.add))
            then(nc.vector.reciprocal(prob[:, 3, :], prob[:, 2, :]))
            then(nc.vector.tensor_tensor(prob[:, 1, :], prob[:, 0, :], prob[:, 3, :], ALU.mult))
            then(nc.vector.scalar_tensor_tensor(prob[:, 2, :], prob[:, 3, :], 1e-9, prob[:, 1, :], ALU.add, ALU.add))
            then(nc.vector.reciprocal(prob[:, 0, :], prob[:, 2, :]))
            nc.vector.tensor_tensor(gate[:, 0, :], prob[:, 3, :], prob[:, 0, :], ALU.mult)
            then(nc.vector.tensor_tensor(gate[:, 1, :], prob[:, 1, :], prob[:, 0, :], ALU.mult))

            def shared_rest(at):
                if at.has(0, 8):
                    wait(dve, s_sil, at.value(1, 1))
                    wait(dve, s_dn, at.value(1, -1))
                    nc.vector.tensor_tensor(aT[at.mod(2)][:], sg[:, at.mod(2), :], u_bank[at.mod(2)][:],
                                            ALU.mult).then_inc(s_act, 1)
                if at.has(-1, 8):
                    wait(dve, s_dn, at.value(1, 0))
                    apart(dve)
                    for half in range(2):
                        xp = X[:, bass.ds(4 * at.batch(-1) + 2 * half, 2), :]
                        last = nc.vector.tensor_tensor(xp, xp, y_bank[at.mod(2, -1)][half][:]
                                                       .rearrange("p (n t) -> p n t", n=2), ALU.add)
                    last.then_inc(s_sh, 1)

            steps(dve, shared_rest, 0, (4, 8), 9, 2)
            dve.wait_ge(s_sc0, 16 * TT)
            ids = rows[:, :, T:T + 1].bitcast(mybir.dt.int32)
            nc.vector.tensor_scalar(ids, ids, TT * P, None, ALU.add).then_inc(s_id1, 1)

            def slot_products(at):
                if at.has(-1, NS):
                    wait(dve, s_si, at.value(1, 0))
                    wait(dve, s_h, at.value(1, -2))
                    nc.vector.tensor_tensor(ar[at.mod(2, -1)][:], sg[:, at.mod(2, -1), 0:I],
                                            up_bank[at.mod(2, -1)][:, I:2 * I], ALU.mult).then_inc(s_a, 1)
                if at.has(-3, NS):
                    wait(dve, s_d, at.value(1, -2))
                    wait(dve, s_put[at.mod(4, -3)], at.turns(-3, 4, 16))
                    nc.vector.tensor_copy(ys[:, at.mod(4, -3), :], down_bank[at.mod(2, -3)][:, 0:T]).then_inc(s_ye, 1)

            steps(dve, slot_products, 0, (8, 80), NS + 3, 8)

            def combine(at):
                m = at.mod(2)
                wait(dve, s_y[m], at.turns(0, 2, 32, 32))
                apart(dve)
                for n in range(4):
                    for k in range(2):
                        xp = X[:, bass.ds(4 * at.batch() + n, 1), :].rearrange("p a t -> p (a t)")
                        last = nc.vector.scalar_tensor_tensor(
                            xp if k == 1 else half_sum[n], pair_in[:, m, k, n, :],
                            gate[:, k, bass.ds(4 * at.batch() + n, 1)],
                            half_sum[n] if k == 1 else xp, ALU.mult, ALU.add)
                        if k == 0:
                            last.then_inc(s_hs, 1)
                            wait(dve, s_hs, at.value(4, n + 1))
                            apart(dve)
                last.then_inc(s_comb, 1)

            steps(dve, combine, 0, (2, 8), 8, 2)

        @block.tensor
        def _(pe):
            pe.wait_ge(s_wd, 32)
            pe.wait_ge(s_w, 48)
            nc.tensor.matmul(bank_a[:, 0:1], w[:, 5, :], bias[:, 5:6], start=True, stop=True).then_inc(s_bo, 1)
            pe.wait_ge(s_beff, 1)

            def held(at, *waits):
                for sem_, value, most in (waits if at.i is None else waits[:1]):
                    wait(pe, sem_, value, most)

            def values(at, group):
                off = -group
                wait(pe, s_exp, at.value(8, 8 * off + 4 * group + 4))
                if group == 0:
                    wait(pe, s_Ve, at.pairs(0, add=1))
                    wait(pe, s_Oe, at.value(1, -1))
                b = at.mod(2, off)
                for chunk in range(2):
                    for j in range(4):
                        h = 4 * group + j
                        last = nc.tensor.matmul(bank_o[b][32 * j:32 * j + 32, T * group:T * group + T],
                                                V[at.odd_pair(off)][:, chunk, b, h, :],
                                                Pr[h][:, T * chunk:T * chunk + T],
                                                start=(chunk == 0), stop=(chunk == 1))
                last.then_inc(s_PV, 1)

            def step(at):
                even = at.r % 2 == 0
                for k in range(H):
                    if at.has(2):
                        c = at.mod(4, 2)
                        if k == 0:
                            v = 32 * ((at.r + 2) // 4 + 1)
                            wait(pe, s_stk[c], v if at.i is None else 32 * at.i + v)
                        wait(pe, s_red, at.value(8, 16 + k - 1))
                        for t in range(2):
                            last = nc.tensor.matmul(bank_s[k % 2][:, T * t:T * t + T],
                                                    Q[c][0:KR, k, P * t:P * t + P], K[c][0:KR, k, :],
                                                    start=True, stop=True)
                        last.then_inc(s_S, 1)
                    if k == 0 and at.has(1):
                        wait(pe, s_msp, at.value(1, 2))
                        if even:
                            held(at, (s_x2, at.pairs(0, add=-1), NP), (s_Ve, at.pairs(0, add=1), NP))
                        else:
                            held(at, (s_BTe, at.pairs(-1), NP), (s_rq, at.pairs(5, add=1), NP), (s_On, at.value(1, -1), NB))
                        bank = (bank_a if even else bank_b)[:].bitcast(BF16)
                        nc.tensor.transpose(bank[0:4 * H, 0:P],
                                            Mb[:, at.mod(2, 1)].rearrange("p a h -> p (a h)"),
                                            ident_b[:]).then_inc(s_TM, 1)
                    if k == 1 and at.has(-1):
                        values(at, 1)
                    if at.has(0):
                        c = at.mod(4)
                        if k == 0:
                            m = at.mod(2)
                            v = 16 * (at.r // 2 + 1)
                            wait(pe, s_mr[m], v if at.i is None else 32 * at.i + v)
                        wait(pe, s_exp, at.value(8, k - 1))
                        for s in range(2):
                            last = nc.tensor.matmul(bank_st[k % 2][:, T * s:T * s + T],
                                                    K[c][0:MROW + 2, k, P * s:P * s + P],
                                                    Q[c][0:MROW + 2, k, :], start=True, stop=True)
                        last.then_inc(s_ST, 1)
                    if even and k == 2 and at.has(6):
                        p = at.odd_pair(6)
                        wait(pe, s_xn, at.pairs(6, add=1))
                        held(at, (s_On, at.value(1, -1), NB), (s_tme, at.value(1, 1), NB), (s_rq, at.pairs(4, add=1), NP))
                        for r in range(2):
                            last = nc.tensor.matmul(bank_b[:, T * r:T * r + T], w[:, r, :], xn[:, p, :],
                                                    start=True, stop=True)
                        last.then_inc(s_qp, 1)
                    if even and k == 3 and at.has(6):
                        p = at.odd_pair(6)
                        v = 16 * ((at.r + 6) // 4 + 1)
                        wait(pe, s_ck[p], v if at.i is None else 16 * at.i + v)
                        held(at, (s_tme, at.value(1, 2), NB), (s_Ve, at.pairs(0, add=1), NP), (s_rk, at.pairs(4, add=1), NP))
                        for r in range(2):
                            last = nc.tensor.matmul(bank_a[:, T * r:T * r + T], w[:, 2 + r, :], ctx_k[:, p, :],
                                                    start=True, stop=True)
                        last.then_inc(s_kp, 1)
                    if k == 4 and at.has(-1):
                        wait(pe, s_Oe, at.value(1, 0))
                        if even:
                            held(at, (s_rq, at.pairs(6, add=1), NP), (s_On, at.value(1, -1), NB))
                        else:
                            held(at, (s_tme, at.value(1, 2), NB), (s_BTe, at.pairs(-1), NP))
                        for t in range(2):
                            for g in range(2):
                                col = P * (2 * t + g)
                                last = nc.tensor.transpose(bank_b[:, col:col + P],
                                                           O[:, T * g + P * t:T * g + P * t + P], ident[:])
                        last.then_inc(s_T1, 1)
                    if k == 5 and at.has(0):
                        values(at, 0)
                    if even and k == 5 and at.has(2):
                        p = at.odd_pair(2)
                        v = 16 * ((at.r + 2) // 4 + 1)
                        wait(pe, s_cv[p], v if at.i is None else 16 * at.i + v)
                        held(at, (s_rk, at.pairs(6, add=1), NP), (s_tme, at.value(1, 2), NB), (s_x2, at.pairs(0, add=-1), NP))
                        for s in range(2):
                            last = nc.tensor.matmul(bank_a[:, P * s:P * s + P], ctx_v[:, p, P * s:P * s + P],
                                                    w[:, 4, :], start=True, stop=True)
                        last.then_inc(s_vp, 1)
                    if even and k == 6 and at.has(-2):
                        wait(pe, s_On, at.value(1, 0))
                        for t in range(2):
                            last = nc.tensor.transpose(bank_b[:, P * t:P * t + P], On[at.odd_pair(-2)][:, t, :], ident[:])
                        last.then_inc(s_BT, 1)
                    if even and k == 7 and at.has(-2):
                        wait(pe, s_BTe, at.pairs(-2, add=1))
                        held(at, (s_Ve, at.pairs(2, add=1), NP), (s_tme, at.value(1, 2), NB))
                        nc.tensor.matmul(bank_a[:, 0:T], w[:, 5, :], OT[:], start=True, stop=True).then_inc(s_WO, 1)

            pe.wait_ge(s_bo, 2)
            pe.wait_ge(s_zero, 19)
            steps(pe, step)

            pe.wait_ge(s_x2, NP)
            pe.wait_ge(s_On, NB)
            pe.wait_ge(s_BTe, NP)
            pe.wait_ge(s_red, H * NB)
            pe.wait_ge(s_exp, H * NB)
            pe.wait_ge(s_Oe, NB)
            pe.wait_ge(s_wx, 16 * 18)

            def tokens(at):
                if at.has(0, TT):
                    wait(pe, s_xts, at.value(1, -1))
                    wait(pe, s_xs, at.value(1, 1))
                    for c in range(2):
                        last = nc.tensor.transpose(tile_bank[at.mod(2)][:, P * c:P * c + P],
                                                   xs[:, at.mod(2), P * c:P * c + P], ident[:])
                    last.then_inc(s_xt, 1)
                if at.has(-1, TT):
                    wait(pe, s_lge, at.value(1, -2))
                    wait(pe, s_xts, at.value(1, 0))
                    for c in range(2):
                        last = nc.tensor.matmul(logit_bank[at.mod(2, -1)][:, 0:E], xTs[at.mod(2, -1)][:, c, :],
                                                wr[:, c, :], start=(c == 0), stop=(c == 1))
                    last.then_inc(s_lg, 1)

            steps(pe, tokens, 0, (4, 32), TT + 1, 2)

            pe.wait_ge(s_mm, 1)
            pe.wait_ge(s_xts, TT)
            nc.tensor.matmul(before_bank[:], low[:, 0, :], MM[:], start=True, stop=True)
            nc.tensor.matmul(all_bank[:], low[:, 1, :], MM[:], start=True, stop=True).then_inc(s_pos, 1)

            def shared(at):
                if at.has(0, 8):
                    wait(pe, s_act, at.value(1, -1))
                    for bank, col in ((g_bank, 0), (u_bank, I)):
                        for c in range(2):
                            last = nc.tensor.matmul(bank[at.mod(2)][:], sgu[:, c, col:col + I],
                                                    XT[:, c, bass.ds(4 * P * at.batch(), 4 * P)],
                                                    start=(c == 0), stop=(c == 1))
                    last.then_inc(s_gu, 1)
                if at.has(-1, 8):
                    wait(pe, s_sh, at.value(1, -2))
                    wait(pe, s_act, at.value(1, 0))
                    for n in range(4):
                        last = nc.tensor.matmul(y_bank[at.mod(2, -1)][n // 2][:, T * (n % 2):T * (n % 2) + T],
                                                aT[at.mod(2, -1)][:, P * n:P * n + P], sd[:], start=True, stop=True)
                    last.then_inc(s_dn, 1)

            pe.wait_ge(s_xte, TT)
            pe.wait_ge(s_slot, 1)
            steps(pe, shared, 0, (4, 8), 9, 2)

            def slot_tile(at):
                if at.has(0, NS):
                    wait(pe, s_te, at.value(1, -1))
                    wait(pe, s_xg[at.mod(8)], at.turns(0, 8, 16, 16))
                    for c in range(2):
                        last = nc.tensor.transpose(tile_bank[at.mod(2)][:, P * c:P * c + P],
                                                   xg[:, at.mod(8), P * c:P * c + P], ident[:])
                    last.then_inc(s_t, 1)
                if at.has(-1, NS):
                    m = at.mod(2, -1)
                    e = pe.value_load(owner[0:1, bass.ds(at.batch(-1), 1)], min_val=0, max_val=E - 1)
                    wait(pe, s_a, at.value(1, -2))
                    wait(pe, s_te, at.value(1, 0))
                    apart(pe)
                    for c in range(2):
                        last = nc.tensor.matmul(up_bank[m][:, 0:2 * I], xTs[m][:, c, :],
                                                wgu[:, bass.ds(e, 1), c, :].rearrange("p a i -> p (a i)"),
                                                start=(c == 0), stop=(c == 1))
                    last.then_inc(s_g, 1)
                if at.has(-2, NS):
                    m = at.mod(2, -2)
                    wait(pe, s_he, at.value(1, -3))
                    wait(pe, s_a, at.value(1, -1))
                    nc.tensor.transpose(mid_bank[m][:, 0:P], ar[m][:], ident[:]).then_inc(s_h, 1)
                if at.has(-3, NS):
                    m = at.mod(2, -3)
                    e = pe.value_load(owner[0:1, bass.ds(at.batch(-3), 1)], min_val=0, max_val=E - 1)
                    wait(pe, s_ye, at.value(1, -4))
                    wait(pe, s_he, at.value(1, -2))
                    apart(pe)
                    nc.tensor.matmul(down_bank[m][:, 0:T], aT[m][:, 0:P],
                                     wd[:, bass.ds(e, 1), :].rearrange("p a t -> p (a t)"),
                                     start=True, stop=True).then_inc(s_d, 1)

            pe.wait_ge(s_sh, 8)
            pe.wait_ge(s_owner, 1)
            steps(pe, slot_tile, 0, (8, 80), NS + 3, 8)


def kernel(**inputs):
    import numpy as np
    import concourse.bacc as bacc
    from concourse.bass_utils import run_bass_kernel_spmd as run

    H, D, T = 8, 8, 256
    x = np.ascontiguousarray(np.asarray(inputs["x"]).reshape(4096, T))
    ctx = np.ascontiguousarray(np.asarray(inputs["ctx_2048"]).reshape(4096, T))

    def by_channel(a, turn=0):
        v = np.asarray(a).reshape(H, D, *np.asarray(a).shape[1:])
        return np.roll(v, -turn, axis=1).swapaxes(0, 1).reshape(np.asarray(a).shape)

    g = {n: np.asarray(inputs["L0_xattn_" + n]) for n in ("Wq", "Wk", "Wv", "Wo", "bq", "bk", "bv", "bo")}
    w6 = np.stack([by_channel(g["Wq"]).T, by_channel(g["Wq"], 4).T, by_channel(g["Wk"]).T,
                   by_channel(g["Wk"], 4).T, g["Wv"].T, g["Wo"].T], axis=1)
    b6 = np.stack([by_channel(g["bq"]), by_channel(g["bq"], 4), by_channel(g["bk"]), by_channel(g["bk"], 4),
                   g["bo"], g["bv"]], axis=1)
    freq = (1.0 / np.float32(10000.0) ** (np.arange(0, D, 2, dtype=np.float32) / np.float32(D))).astype(np.float32)
    ang = np.arange(T, dtype=np.float32)[None, :] * np.tile(freq, 2)[:, None]
    sign = np.where(np.arange(D) < D // 2, -1.0, 1.0).astype(np.float32)[:, None]
    one = np.stack([np.cos(ang), np.sin(ang) * sign], axis=1).astype(np.float32)
    rope = np.tile(np.repeat(one, H, axis=0), (2, 1, 1))

    arrays = {"x_dram": x, "ctx_dram": ctx, "w6": np.ascontiguousarray(w6),
              "bias6": np.ascontiguousarray(np.tile(b6, (2, 1))), "rope": np.ascontiguousarray(rope),
              "ident_dram": np.eye(128, dtype=np.float32)}
    m = {n: np.asarray(inputs["L0_ffn_" + n]) for n in ("Wr", "bias", "Wg", "Wu", "Wd", "sWg", "sWu", "sWd")}
    E, P = 16, 128
    counts = np.concatenate([np.arange(E) - 1024.0, np.arange(32) * 128.0, np.arange(80),
                             np.tril(np.ones((E, E))).reshape(-1)]).astype(np.float32)
    below = np.stack([np.triu(np.ones((P, P)), 1), np.ones((P, P))], axis=1).astype(np.float32)
    arrays |= {
        "w_router": np.ascontiguousarray(m["Wr"].T), "b_router": np.tile(m["bias"][None], (P, 1)),
        "w_gu": np.concatenate([m["Wg"], m["Wu"]], axis=2), "w_down": np.ascontiguousarray(m["Wd"]),
        "s_gu": np.concatenate([m["sWg"], m["sWu"]], axis=1), "s_down": np.ascontiguousarray(m["sWd"]),
        "counts": np.tile(counts, (P, 1)), "below": below,
    }
    nc = bacc.Bacc("TRN2", target_bir_lowering=False, num_devices=1)
    args = [nc.dram_tensor(n, a.shape, mybir.dt.from_np(a.dtype), kind="ExternalInput").ap() for n, a in arrays.items()]
    out = nc.dram_tensor("out", (4096, T), F32, kind="ExternalOutput").ap()
    xattn_moe(nc, *args, out)
    r = run(nc, [arrays], core_ids=[0])
    return r.results[0]["out"].reshape(64, 64, T)
```

```python
from contextlib import ExitStack

import concourse.bass as bass
from concourse import mybir

ALU = mybir.AluOpType
ACT = mybir.ActivationFunctionType
AX = mybir.AxisListType
F32 = mybir.dt.float32
BF16 = mybir.dt.bfloat16
I32 = mybir.dt.int32


class Step:

    def __init__(self, r, i=None, turn=4):
        self.r, self.i, self.turn = r, i, turn

    def batch(self, off=0):
        return self.r + off if self.i is None else self.turn * self.i + (self.r + off)

    def pair(self, off=0):
        h = (self.r + off) // 2
        return h if self.i is None else self.turn // 2 * self.i + h

    def mod(self, n, off=0):
        return (self.r + off) % n

    def odd_pair(self, off=0):
        return (self.r + off) // 2 % 2

    def value(self, per_batch, add):
        v = per_batch * self.r + add
        return v if self.i is None else (self.turn * per_batch) * self.i + v

    def pairs(self, off, per=1, add=0):
        v = per * ((self.r + off) // 2) + add
        return v if self.i is None else (self.turn // 2 * per) * self.i + v

    def turns(self, off, n, per, add=0):
        v = per * ((self.r + off) // n) + add
        return v if self.i is None else (self.turn // n * per) * self.i + v

    def has(self, off, n=64):
        return self.i is not None or 0 <= self.r + off < n


def wait(eng, sem, value, most=None):
    if isinstance(value, int):
        if most is not None:
            value = min(value, most)
        if value <= 0:
            return
    eng.wait_ge(sem, value)


def xattn_moe(nc, x, ctx_in, w6, bias6, rope, ident_in, w_router, b_router, w_gu, w_down, shared_gu, shared_down, counts, below, out):
    NB, C, T = 64, 64, 256
    P = 128
    H, D = 8, 8
    NP = NB // 2
    PARTS = 3
    KR = PARTS * PARTS * D
    MROW = 96
    SCALE = float(D) ** -0.5
    EPS = 1e-5
    E, I = 16, 128
    TT = NP
    NS = 80
    ROW = T + 4
    BIG = 1024.0

    slots = nc.dram_tensor("slots", (NS * P, ROW), F32, kind="Internal").ap()
    results = nc.dram_tensor("results", (2 * TT * P, T), F32, kind="Internal").ap()
    SLOTS = PARTS + 2 * PARTS - 1
    scratch = nc.dram_tensor("parts", (NB, SLOTS, C, T), BF16, kind="Internal").ap()

    with ExitStack() as stack:
        def sb(name, shape, dt=F32):
            return stack.enter_context(nc.sbuf_tensor(name, shape, dt))

        def psum(name):
            return stack.enter_context(nc.psum_tensor(name, [P, 512], F32))

        def sem(name):
            return stack.enter_context(nc.semaphore(name))

        X = sb("X", [P, NP, T])
        ctx_kv = sb("ctx_kv", [P, 4, T])
        ctx_k, ctx_v = ctx_kv[:, 0:2], ctx_kv[:, 2:4]
        w = sb("w", [P, 6, P])
        bias = sb("bias", [P, 6])
        beff = sb("beff", [P, 1])
        tab = sb("tab", [P, 2, T])
        ident = sb("ident", [P, P])
        ident_b = sb("ident_b", [P, P], BF16)
        eps = sb("eps", [P, 1])
        st1 = sb("st1", [P, 2, 6])
        mv1 = sb("mv1", [P, NP, 2])
        std1 = sb("std1", [P, NP])
        rstd1 = sb("rstd1", [P, NP])
        xn = sb("xn", [P, 2, T])
        work = sb("work", [P, 4, 2, T])
        rc, rs, qk, rest = [work[:, i] for i in range(4)]
        parts_sb = sb("parts_sb", [P, 2 * 2 * PARTS * T], BF16)
        parts = parts_sb[:].rearrange("p (n s k t) -> p n s k t", n=2, s=2, k=PARTS)
        QK = sb("QK", [P, 8, H, T], BF16)
        Q = [QK[:, i] for i in range(4)]
        K = [QK[:, 4 + i] for i in range(4)]
        M = sb("M", [P, 2, 2 * H])
        Mb = sb("Mb", [P, 2, 2, 2 * H], BF16)
        Mt = sb("Mt", [4 * H, 2, P], BF16)
        wide = sb("wide", [P, 8 * ROW])
        V = [wide[:, 1024 * i:1024 * i + 1024].rearrange("p (s b h e) -> p s b h e", s=2, b=2, h=H) for i in range(2)]
        Pr = [sb(f"Pr{i}", [P, 2 * T]) for i in range(H)]
        O = sb("O", [P, 2 * T])
        rden = sb("rden", [P, 16])
        On = [sb(f"On{i}", [P, 2, P]) for i in range(2)]
        OT = sb("OT", [P, T])
        st2 = sb("st2", [P, 6])
        mv2 = sb("mv2", [P, 2, 2])
        vv = sb("vv", [P, 2, 4])
        newton = sb("newton", [P, 2])

        rows = sb("rows", [P, TT, ROW])
        xT_sb = sb("xT_sb", [P, 2 * T + 4])
        xTs = [xT_sb[:, T * i:T * i + T].rearrange("p (c n) -> p c n", c=2) for i in range(2)]
        blank = xT_sb[:, T:T + ROW]
        xs = sb("xs", [P, T])
        wr = sb("wr", [P, 2, E])
        wgu = sb("wgu", [P, E, 2, 2 * I])
        wd = sb("wd", [P, E, T])
        late = parts_sb[:].bitcast(F32)
        sgu = late[:, 0:512].rearrange("p (c i) -> p c i", c=2)
        sd = late[:, 512:768]
        cnt = late[:, 768:1152]
        low = late[:, 1152:1408].rearrange("p (a n) -> p a n", a=2)
        br = sb("br", [P, E])
        LG = sb("LG", [P, TT * E])
        GE, OH0, OH1, MM, PA, PB, PC = [Pr[i] for i in range(7)]
        slot = sb("slot", [P, 2, TT], mybir.dt.int32)
        prob = On[0][:, 0, :].rearrange("p (k n) -> p k n", n=TT)
        nt = On[0][:, 1, 0:4 * E].rearrange("p (k e) -> p k e", e=E)
        slot_f = On[0][:, 1, 4 * E:4 * E + 2 * TT].rearrange("p (k n) -> p k n", n=TT)
        m1, ix = [On[1][:, 0, 2 * TT * i:2 * TT * i + 2 * TT].rearrange("p (k n) -> p k n", n=TT) for i in range(2)]
        gate = On[1][:, 1, 0:2 * TT].rearrange("p (k n) -> p k n", n=TT)
        owner_f = sb("owner_f", [1, NS])
        owner = sb("owner", [1, NS], mybir.dt.int32)
        xg = wide[:].rearrange("p (a t) -> p a t", a=8)
        sg = work[:, 0:2].rearrange("p a b t -> p a (b t)")
        aT = [work[:, 2 + i].rearrange("p b t -> p (b t)") for i in range(2)]
        ar = [OT[:, P * i:P * i + P] for i in range(2)]
        pair_in = QK[:].bitcast(F32).rearrange("p a h t -> p (a h t)")[:, 0:16 * T].rearrange(
            "p (m k n t) -> p m k n t", m=2, k=2, n=4)
        half_sum = [Pr[4 + n // 2][:, T * (n % 2):T * (n % 2) + T] for n in range(4)]
        ys = ctx_kv

        bank_s = [psum(f"bank_s{i}") for i in range(3)]
        bank_st = [psum(f"bank_st{i}") for i in range(2)]
        bank_o = psum("bank_o")
        bank_a = psum("bank_a")
        bank_b = psum("bank_b")
        tile_bank = (bank_a, bank_b)
        before_bank, all_bank = bank_a, bank_b
        up_bank, mid_bank, down_bank = bank_st, (bank_o, bank_s[2]), bank_s[0:2]
        S_BANK = ((0, 1, 2, 0, 1, 2, 0, 1), (2, 0, 1, 2, 0, 1, 2, 1))
        taken = S_BANK[0] + S_BANK[1]
        S_BACK = [[next(d for d in range(1, 9) if taken[H * m + k - d] == taken[H * m + k]) for k in range(H)]
                  for m in range(2)]

        s_x = [sem(f"s_xin{g}") for g in range(8)]
        s_w = sem("s_w")
        s_zero = sem("s_zero")
        s_wd = sem("s_wd")
        s_ck = [sem(f"s_ck{i}") for i in range(2)]
        s_cv = [sem(f"s_cv{i}") for i in range(2)]
        s_ptw = [sem(f"s_ptw{i}") for i in range(4)]
        s_stk = [sem(f"s_stk{i}") for i in range(4)]
        s_mr = [sem(f"s_mr{i}") for i in range(2)]
        s_st1 = sem("s_st1")
        s_mv1 = sem("s_mv1")
        s_std1 = sem("s_std1")
        s_rstd1 = sem("s_rstd1")
        s_xn = sem("s_xn")
        s_proj = sem("s_proj")
        s_vp = sem("s_vp")
        s_rope = sem("s_rope")
        s_qk = sem("s_qk")
        s_p1 = sem("s_p1")
        s_r1 = sem("s_r1")
        s_p2 = sem("s_p2")
        s_pt = sem("s_pt")
        s_S = sem("s_S")
        s_red = sem("s_red")
        s_hi = sem("s_hi")
        s_msp = sem("s_msp")
        s_TM = sem("s_TM")
        s_tme = sem("s_tme")
        s_ST = sem("s_ST")
        s_exp = sem("s_exp")
        s_PV = sem("s_PV")
        s_Ve = sem("s_Ve")
        s_Oe = sem("s_Oe")
        s_T1 = sem("s_T1")
        s_rc = sem("s_rc")
        s_On = sem("s_On")
        s_BT = sem("s_BT")
        s_BTe = sem("s_BTe")
        s_WO = sem("s_WO")
        s_x2 = sem("s_x2")
        s_st2 = sem("s_st2")
        s_guess = sem("s_guess")
        s_nw = sem("s_nw")
        s_vv = sem("s_vv")
        s_sh2 = sem("s_sh2")
        s_mv2 = sem("s_mv2")
        s_bo = sem("s_bo")
        s_beff = sem("s_beff")
        s_wx = sem("s_wx")
        s_wr = sem("s_wr")
        s_blank = sem("s_blank")
        s_fill = sem("s_fill")
        s_id = sem("s_id")
        s_xs = sem("s_xs")
        s_xcp = sem("s_xcp")
        s_xt = sem("s_xt")
        s_xte = sem("s_xte")
        s_lg = sem("s_lg")
        s_lge = sem("s_lge")
        s_mm = sem("s_mm")
        s_pos = sem("s_pos")
        s_ex = sem("s_ex")
        s_rt = sem("s_rt")
        s_slot = sem("s_slot")
        s_first = [sem(f"s_first{i}") for i in range(2)]
        s_owner = sem("s_owner")
        s_sh = sem("s_sh")
        s_in = sem("s_in")
        s_t = sem("s_t")
        s_te = sem("s_te")
        s_g = sem("s_g")
        s_si = sem("s_si")
        s_a = sem("s_a")
        s_h = sem("s_h")
        s_he = sem("s_he")
        s_d = sem("s_d")
        s_ye = sem("s_ye")
        s_comb = sem("s_comb")
        s_hs = sem("s_hs")
        s_second = sem("s_second")
        s_xg = [sem(f"s_xg{i}") for i in range(8)]
        s_put = [sem(f"s_put{i}") for i in range(4)]
        s_y = [sem(f"s_y{i}") for i in range(2)]
        s_o = [sem(f"s_o{i}") for i in range(2)]

        FIRST, LAST = -8, 69
        LOOP = (8, 56)

        def steps(eng, step, first=FIRST, loop=LOOP, last=LAST, turn=4):
            for b in range(first, loop[0]):
                step(Step(b, None, turn))
            with eng.Fori(loop[0] // turn, loop[1] // turn) as i:
                for r in range(turn):
                    step(Step(r, i, turn))
            for b in range(loop[1], last):
                step(Step(b, None, turn))

        def implied(eng, at, sem_, value):
            if at.i is None:
                wait(eng, sem_, value)


        def apart(eng):
            eng.wait_ge(s_w, 48)

        block = stack.enter_context(nc.Block())

        @block.sync
        def _(sp):
            for g in range(2):
                sp.dma_start(X[:, 4 * g:4 * g + 4, :],
                             x.rearrange("(n p) t -> p n t", p=P)[:, 4 * g:4 * g + 4, :]).then_inc(s_x[g], 16)
            sp.dma_start(bias[:], bias6).then_inc(s_w, 16)
            sp.dma_start(tab[:], rope).then_inc(s_w, 16)
            sp.dma_start(ident[:], ident_in).then_inc(s_w, 16)
            sp.wait_ge(s_zero, 1)
            sp.dma_start(w[0:C, :, 0:C], w6).then_inc(s_wd, 16)
            sp.dma_start(w[C:P, :, C:P], w6).then_inc(s_wd, 16)
            for g in range(2, 8):
                sp.dma_start(X[:, 4 * g:4 * g + 4, :],
                             x.rearrange("(n p) t -> p n t", p=P)[:, 4 * g:4 * g + 4, :]).then_inc(s_x[g], 16)
            sp.wait_ge(s_zero, 13)

            def alone(sem_, value):
                wait(sp, sem_, known(value))

            def known(index):
                if not isinstance(index, int):
                    sp.compute_val(index)
                return index

            def load(dst, sems, at, off, pair):
                p = at.odd_pair(off)
                sp.dma_start(dst[:, p:p + 1, :].rearrange("p a t -> p (a t)"),
                             ctx_in.rearrange("(n p) t -> n p t", p=P)[bass.ds(pair, 1), :, :]
                             .rearrange("n p t -> (n p) t")).then_inc(sems[p], 16)

            def weights(n):
                e = 4 * n
                if n == 0:
                    sp.dma_start(wr[:], w_router.rearrange("(c p) i -> p c i", p=P)).then_inc(s_wr, 16)
                    sp.dma_start(br[:], b_router).then_inc(s_wr, 16)
                for c in range(2):
                    sp.dma_start(wgu[:, e:e + 4, c, :],
                                 w_gu.rearrange("e (c p) i -> p e c i", p=P)[:, e:e + 4, c, :]).then_inc(s_wx, 16)
                sp.dma_start(wd[:, e:e + 4, :], w_down[e:e + 4].rearrange("e p t -> p e t")).then_inc(s_wx, 16)

            def late_weights():
                for n in range(4):
                    sp.wait_ge(s_ptw[n], (32, 64)[n % 2] * NP // 2)
                sp.dma_start(sgu, shared_gu.rearrange("(c p) i -> p c i", p=P)).then_inc(s_wx, 16)
                for dst, src in ((sd, shared_down), (cnt, counts), (low, below)):
                    sp.dma_start(dst, src).then_inc(s_wx, 16)

            def fill(n):
                alone(s_blank, 2)
                sp.dma_start(slots.rearrange("(n p) t -> p n t", p=P)[:, 10 * n:10 * n + 10, :],
                             blank.rearrange("p (o t) -> p o t", o=1).to_broadcast([P, 10, ROW])).then_inc(s_fill, 16)

            def step(at):
                if at.i is None and 0 <= at.r < 4:
                    weights(at.r)
                if at.i is None and 56 <= at.r < 64:
                    fill(at.r - 56)
                if at.i is None and at.r == 62:
                    late_weights()
                if at.r % 2 == 0 and at.has(8):
                    pair = known(at.pair(8))
                    alone(s_proj, at.value(1, 6))
                    load(ctx_k, s_ck, at, 8, pair)
                if at.r % 2 == 0 and at.has(4):
                    pair = known(at.pair(4))
                    alone(s_vp, at.pairs(4, add=-1))
                    load(ctx_v, s_cv, at, 4, pair)
                if at.has(3):
                    batch = known(at.batch(3))
                    c = at.mod(4, 3)
                    q_written, k_written = known(at.turns(3, 4, 32, 32)), known(at.turns(3, 4, 64, 64))
                    used = known(at.value(8, 0))
                    alone(s_ptw[2 * at.odd_pair(3)], q_written)
                    alone(s_ptw[2 * at.odd_pair(3) + 1], k_written)
                    alone(s_ST, used)
                    src = scratch[bass.ds(batch, 1)].rearrange("a s c t -> (a s) (c t)")
                    for dst, slot, turn in ((Q[c], 0, 0), (K[c], PARTS, C * T)):
                        g = src[slot:slot + 1]
                        rows = [[turn, PARTS], [H * T, PARTS * D], [1, H * T]]
                        sp.dma_start(dst[0:KR].rearrange("r h t -> r (h t)"),
                                     bass.AP(tensor=g.tensor, offset=g.offset, ap=rows)).then_inc(s_stk[c], 16)
                if at.has(1):
                    alone(s_tme, at.value(1, 2))
                    c = at.mod(4, 1)
                    m = at.mod(2, 1)
                    sp.dma_start(Q[c][MROW:MROW + 2].rearrange("r h t -> r (h t)"), Mt[:, m, :]).then_inc(s_mr[m], 16)
                if at.has(5):
                    pair = known(at.pair(5))
                    alone(s_pt, at.value(1, 6))
                    n, qk_ = at.mod(4, 5), at.mod(2, 5)
                    dst = scratch.rearrange("(n b) s c t -> n b c s t", b=2)
                    for half in range(2):
                        to = dst[bass.ds(pair, 1), half:half + 1].rearrange("n b c s t -> (n b c) s t")
                        own = parts[C * half:C * half + C, at.odd_pair(5), qk_]
                        sp.dma_start(to[:, PARTS * qk_:PARTS * qk_ + PARTS], own).then_inc(s_ptw[n], 16)
                        if qk_:
                            sp.dma_start(to[:, 2 * PARTS:SLOTS], own[:, 0:PARTS - 1, :]).then_inc(s_ptw[n], 16)

            steps(sp, step)

            def feed(at):
                if at.has(0, NS):
                    tile, read, sent = known(at.batch()), known(at.value(1, TT - 7)), known(at.turns(-8, 4, 16, 16))
                    if at.i is not None or at.r >= 8:
                        alone(s_t, read)
                    alone(s_put[at.mod(4)], sent)
                    sp.dma_start(xg[:, at.mod(8), :],
                                 slots.rearrange("(n p) t -> n p t", p=P)[bass.ds(tile, 1)]
                                 .rearrange("n p t -> (n p) t")).then_inc(s_xg[at.mod(8)], 16)

            sp.wait_ge(s_second, 16 * TT)
            sp.wait_ge(s_owner, 1)
            steps(sp, feed, 0, (8, 72), NS, 8)

            for i in range(4):
                sp.wait_ge(s_put[i], 16 * (NS // 4))
            res = results[0:2 * TT * P].rearrange("(k g n p) t -> p g k n t", k=2, n=4, p=P)

            def gather(at):
                if at.has(0, TT // 4):
                    g, m = known(at.batch()), at.mod(2)
                    used = known(at.value(1, -1))
                    alone(s_comb, used)
                    for k in range(2):
                        sp.dma_start(pair_in[:, m, k], res[:, bass.ds(g, 1), k].rearrange("p g n t -> p (g n) t")).then_inc(s_y[m], 16)
                if at.has(-1, TT // 4):
                    g, m = known(at.batch(-1)), at.mod(2, -1)
                    made = known(at.value(1, 0))
                    alone(s_comb, made)
                    sp.dma_start(out.rearrange("(g n p) t -> p g n t", n=4, p=P)[:, bass.ds(g, 1)].rearrange("p g n t -> p (g n) t"),
                                 X[:, bass.ds(4 * g, 4), :]).then_inc(s_o[m], 16)

            steps(sp, gather, 0, (2, 8), 9, 2)
            for i in range(2):
                sp.wait_ge(s_o[i], 16 * 4)

        @block.gpsimd
        def _(pool):
            pieces = [(w[:], 0.0)]
            for i in range(4):
                pieces += [(Q[i][64:P], 0.0), (K[i][64:MROW], 0.0), (K[i][MROW:P], -1.0)]
            for i in range(2):
                pieces += [(V[i][:, :, :, :, 0:8], 0.0), (V[i][:, :, :, :, 9:32], 0.0), (V[i][:, :, :, :, 8:9], 1.0)]
            nc.gpsimd.memset(blank, 0.0).then_inc(s_blank, 1)
            pool.wait_ge(s_blank, 1)
            nc.gpsimd.iota(xT_sb[:, 2 * T:2 * T + 1].bitcast(mybir.dt.int32), pattern=[[0, 1]], base=2 * TT * P,
                           channel_multiplier=1).then_inc(s_blank, 1)
            pool.wait_ge(s_blank, 2)
            for n, (piece, fill) in enumerate(pieces):
                wait(pool, s_zero, n)
                nc.gpsimd.memset(piece, fill).then_inc(s_zero, 1)

            def step(at):
                if at.has(6):
                    p, h = at.odd_pair(6), at.mod(2)
                    wait(pool, s_rope, at.value(1, 7))
                    wait(pool, s_pt, at.value(1, 5))
                    nc.gpsimd.tensor_tensor(qk[:, h], rc[:, h], rs[:, h], ALU.add).then_inc(s_qk, 1)
                    wait(pool, s_ptw[at.mod(4, 6)], at.turns(6, 4, 64 if h else 32))
                    nc.gpsimd.tensor_tensor(parts[:, p, h, 0, :], rc[:, h], rs[:, h], ALU.add).then_inc(s_p1, 1)
                    wait(pool, s_p1, at.value(1, 7))
                    nc.gpsimd.tensor_tensor(rest[:, h], qk[:, h], parts[:, p, h, 0, :], ALU.subtract).then_inc(s_r1, 1)
                    nc.gpsimd.tensor_tensor(parts[:, p, h, 1, :], qk[:, h], parts[:, p, h, 0, :],
                                            ALU.subtract).then_inc(s_p2, 1)
                    wait(pool, s_p2, at.value(1, 7))
                    nc.gpsimd.tensor_tensor(parts[:, p, h, 2, :], rest[:, h], parts[:, p, h, 1, :],
                                            ALU.subtract).then_inc(s_pt, 1)
                if at.r % 2 == 1 and at.has(-3):
                    p = at.odd_pair(-3)
                    half, y, t = vv[:, p, 1:2], vv[:, p, 3:4], newton[:, 0:1]
                    wait(pool, s_guess, at.pairs(-3, add=1))
                    n = 0
                    for _ in range(3):
                        for dst, a, b, op in ((t, y, y, ALU.mult), (t, t, half, ALU.mult),
                                              (t, newton[:, 1:2], t, ALU.subtract), (y, y, t, ALU.mult)):
                            wait(pool, s_nw, at.pairs(-3, 12, n))
                            nc.gpsimd.tensor_tensor(dst, a, b, op).then_inc(s_nw, 1)
                            n += 1

            steps(pool, step)

            ids = rows[:, :, T:T + 1].bitcast(mybir.dt.int32)
            nc.gpsimd.iota(ids, pattern=[[P, TT], [0, 1]], base=0, channel_multiplier=1).then_inc(s_id, 1)
            nc.gpsimd.memset(rows[:, :, T + 1:ROW], 0.0).then_inc(s_id, 1)

            pool.wait_ge(s_slot, 1)
            pool.wait_ge(s_id, 2)
            pool.wait_ge(s_fill, 16 * 8)
            def scatter(k, half, done):
                for n in range(TT // 2 * half, TT // 2 * (half + 1)):
                    pool.indirect_dma_start(
                        out=slots, out_offset=bass.IndirectOffsetOnAxis(ap=slot[:, k, n:n + 1], axis=0),
                        in_=rows[:, n, :], in_offset=None).then_inc(done, 16)

            for half in range(2):
                scatter(0, half, s_first[half])
            for half in range(2):
                pool.wait_ge(s_first[half], 16 * TT // 2)
                nc.gpsimd.iota(ids[:, TT // 2 * half:TT // 2 * (half + 1)], pattern=[[P, TT // 2], [0, 1]],
                               base=TT * P + TT // 2 * P * half, channel_multiplier=1).then_inc(s_id, 1)
                pool.wait_ge(s_id, 3 + half)
                scatter(1, half, s_second)

            def put(at):
                if at.has(-4, NS):
                    if at.i is not None:
                        pool.compute_val(at.value(1, TT - 3))
                    apart(pool)
                    wait(pool, s_ye, at.value(1, TT - 3))
                    pool.indirect_dma_start(
                        out=results, out_offset=bass.IndirectOffsetOnAxis(
                            ap=xg[:, at.mod(8, -4), T:T + 1].bitcast(mybir.dt.int32), axis=0),
                        in_=ys[:, at.mod(4), :], in_offset=None,
                        bounds_check=2 * TT * P - 1, oob_is_err=False).then_inc(s_put[at.mod(4)], 16)

            steps(pool, put, 0, (8, 80), NS + 4, 8)

        @block.scalar
        def _(act):
            act.wait_ge(s_mv1, 4)
            act.wait_ge(s_w, 48)
            act.wait_ge(s_beff, 1)
            nc.scalar.activation(std1[:, 0:4], mv1[:, 0:4, 1], ACT.Sqrt, bias=eps[:, 0:1]).then_inc(s_std1, 1)
            act.wait_ge(s_mv1, NP)
            nc.scalar.activation(std1[:, 4:NP], mv1[:, 4:NP, 1], ACT.Sqrt, bias=eps[:, 0:1]).then_inc(s_std1, 1)

            def step(at):
                for k in range(H):
                    if at.has(0):
                        wait(act, s_ST, at.value(8, k + 1))
                        if k % 4 == 0:
                            wait(act, s_PV, at.value(2, -1 + k // 4))
                        nc.scalar.activation(Pr[k][:], bank_st[k % 2][:], ACT.Exp, scale=SCALE).then_inc(s_exp, 1)
                    if k == 2 and at.has(1):
                        m = at.mod(2, 1)
                        wait(act, s_TM, at.value(1, 2))
                        wait(act, s_mr[m], at.turns(1, 2, 16))
                        nc.scalar.activation(Mt[:, m, :], bank_a[:].bitcast(BF16)[0:4 * H, 0:P], ACT.Copy).then_inc(s_tme, 1)
                    if k == 2 and at.has(-1):
                        wait(act, s_PV, at.value(2, 0))
                        wait(act, s_T1, at.value(1, -1))
                        nc.scalar.activation(O[:], bank_o[:], ACT.Copy).then_inc(s_Oe, 1)
                    if k == 0 and at.r % 2 == 1 and at.has(1):
                        wait(act, s_vp, at.pairs(1, add=1))
                        wait(act, s_PV, at.pairs(1, 4, -4))
                        nc.scalar.activation(
                            V[at.odd_pair(1)][:].rearrange("p s b h e -> p (s b h) e")[:, :, 0:D],
                            bank_a[:].rearrange("p (g e) -> p g e", e=D)[:, 0:32, :], ACT.Copy).then_inc(s_Ve, 1)
                    if k == 7 and at.r % 2 == 0 and at.has(-2):
                        wait(act, s_BT, at.pairs(-2, add=1))
                        wait(act, s_WO, at.pairs(-2))
                        nc.scalar.activation(OT[:], bank_b[:, 0:T], ACT.Copy).then_inc(s_BTe, 1)
                    if k == 3 and at.r % 2 == 1 and at.has(-5):
                        wait(act, s_xs, at.pairs(-5, add=1))
                        apart(act)
                        nc.scalar.activation(rows[:, bass.ds(at.pair(-5), 1), 0:T].rearrange("p a t -> p (a t)"),
                                             xs[:], ACT.Copy).then_inc(s_xcp, 1)
                    if k == 0 and at.r % 2 == 0 and at.has(-6):
                        wait(act, s_xt, at.pairs(-6, add=1))
                        wait(act, s_lg, at.pairs(-6))
                        nc.scalar.activation(xTs[0][:], bank_b[:, 0:2 * P].rearrange("p (c n) -> p c n", c=2),
                                             ACT.Copy).then_inc(s_xte, 1)

            steps(act, step)

            act.wait_ge(s_ex, 1)
            nc.scalar.activation(PC[:], PB[:], ACT.Exp).then_inc(s_ex, 1)
            nc.scalar.activation(prob[:, 0, :], prob[:, 1, :], ACT.Exp).then_inc(s_ex, 1)

            def tile(at, n, base):
                if at.has(0, n):
                    implied(act, at, s_g, at.value(1, base - 1))
                    wait(act, s_t, at.value(1, base + 1))
                    nc.scalar.activation(xTs[at.mod(2)][:], tile_bank[at.mod(2)][:, 0:2 * P]
                                         .rearrange("p (c n) -> p c n", c=2), ACT.Copy).then_inc(s_te, 1)
                if at.has(-3, n):
                    implied(act, at, s_d, at.value(1, base - 4))
                    wait(act, s_h, at.value(1, base - 2))
                    nc.scalar.activation(aT[at.mod(2, -3)][:, 0:P], mid_bank[at.mod(2, -3)][:, 0:P],
                                         ACT.Copy).then_inc(s_he, 1)
                if at.has(-1, n):
                    implied(act, at, s_a, at.value(1, base - 2))
                    wait(act, s_g, at.value(1, base))
                    nc.scalar.activation(sg[:, at.mod(2, -1), 0:I], up_bank[at.mod(2, -1)][:, 0:I],
                                         ACT.Silu).then_inc(s_si, 1)

            def shared(at):
                tile(at, TT, 0)
                if at.has(1, TT):
                    wait(act, s_t, at.value(1, 0))
                    apart(act)
                    nc.scalar.activation(xn[:, at.mod(2, 1), :], rows[:, bass.ds(at.batch(1), 1), 0:T]
                                         .rearrange("p a t -> p (a t)"), ACT.Copy).then_inc(s_in, 1)

            act.wait_ge(s_xcp, NP)
            act.wait_ge(s_fill, 16 * 8)
            steps(act, shared, -1, (6, 30), TT + 3, 2)
            steps(act, lambda at: tile(at, NS, TT), 0, (8, 80), NS + 3, 8)

        @block.vector
        def _(dve):
            nc.vector.memset(eps[:], EPS)
            nc.vector.memset(newton[:, 1:2], 1.5)
            dve.wait_ge(s_w, 48)
            nc.vector.tensor_copy(ident_b[:], ident[:]).then_inc(s_bo, 1)
            dve.wait_ge(s_bo, 2)
            nc.vector.tensor_tensor(beff[:], bank_a[:, 0:1], bias[:, 4:5], ALU.add).then_inc(s_beff, 1)

            def stats(p):
                if p >= 2:
                    dve.wait_ge(s_mv1, p - 1)
                nc.vector.bn_stats(st1[:, p % 2, :], X[:, p, :]).then_inc(s_st1, 1)
                dve.wait_ge(s_st1, p + 1)
                nc.vector.bn_aggr(mv1[:, p, :], st1[:, p % 2, :]).then_inc(s_mv1, 1)

            dve.wait_ge(s_x[0], 16)
            for p in range(4):
                stats(p)
            dve.wait_ge(s_std1, 1)
            nc.vector.reciprocal(rstd1[:, 0:4], std1[:, 0:4]).then_inc(s_rstd1, 1)

            def rest_of_stats():
                for p in range(4, NP):
                    if p % 4 == 0:
                        dve.wait_ge(s_x[p // 4], 16)
                    stats(p)
                dve.wait_ge(s_std1, 2)
                nc.vector.reciprocal(rstd1[:, 4:NP], std1[:, 4:NP]).then_inc(s_rstd1, 1)

            def step(at):
                for k in range(H):
                    if at.r % 2 == 1 and at.has(-3) and k == 2:
                        wait(dve, s_x2, at.pairs(-3, add=1))
                    if at.r % 2 == 1 and at.has(-3) and k == 3:
                        wait(dve, s_st2, at.pairs(-3, add=1))
                    if at.has(2):
                        c = at.mod(2)
                        wait(dve, s_S, at.value(8, 16 + k + 1))
                        if k == 0:
                            wait(dve, s_msp, at.value(1, 1))
                        nc.vector.tensor_reduce(M[:, c, 2 * k:2 * k + 2],
                                                bank_s[S_BANK[c][k]][:].rearrange("p (a s) -> p a s", a=2),
                                                AX.X, ALU.max).then_inc(s_red, 1)
                    if k == 0 and at.has(1):
                        c = at.mod(2, 1)
                        wait(dve, s_red, at.value(8, 16))
                        wait(dve, s_TM, at.value(1, 0))
                        nc.vector.tensor_copy(Mb[:, c, 0, :], M[:, c, :]).then_inc(s_hi, 1)
                        wait(dve, s_hi, at.value(1, 2))
                        nc.vector.tensor_tensor(Mb[:, c, 1, :], M[:, c, :], Mb[:, c, 0, :],
                                                ALU.subtract).then_inc(s_msp, 1)
                    if k == 1 and at.r % 2 == 0 and at.has(6):
                        p = at.odd_pair(6)
                        pair = at.pair(6)
                        dve.wait_ge(s_rstd1, 1 if at.i is None and pair < 4 else 2)
                        wait(dve, s_proj, at.value(1, 3))
                        nc.vector.tensor_scalar(
                            xn[:, p, :], X[:, bass.ds(pair, 1), :].rearrange("p a t -> p (a t)"),
                            mv1[:, bass.ds(pair, 1), 0:1].rearrange("p a t -> p (a t)"),
                            rstd1[:, bass.ds(pair, 1)], ALU.subtract, ALU.mult).then_inc(s_xn, 1)
                    if k == 1 and at.r % 2 == 1 and at.has(-3):
                        pair = at.pair(-3)
                        xp = X[:, bass.ds(pair, 1), :].rearrange("p a t -> p (a t)")
                        wait(dve, s_WO, at.pairs(-3, add=1))
                        nc.vector.scalar_tensor_tensor(xp, bank_b[:, 0:T], beff[:, 0:1], xp,
                                                       ALU.add, ALU.add).then_inc(s_x2, 1)
                    if k == 2 and at.r % 2 == 1 and at.has(-3):
                        nc.vector.bn_stats(st2[:], X[:, bass.ds(at.pair(-3), 1), :]
                                           .rearrange("p a t -> p (a t)")).then_inc(s_st2, 1)
                    if at.r % 2 == 1 and at.has(-3):
                        p = at.odd_pair(-3)
                        v = vv[:, p]
                        if k == 3:
                            nc.vector.bn_aggr(mv2[:, p, :], st2[:]).then_inc(s_mv2, 1)
                        if k == 4:
                            wait(dve, s_mv2, at.pairs(-3, add=1))
                            nc.vector.tensor_scalar(v[:, 0:1], mv2[:, p, 1:2], EPS, None, ALU.add).then_inc(s_vv, 1)
                        if k == 5:
                            wait(dve, s_vv, at.pairs(-3, add=1))
                            nc.vector.tensor_scalar(v[:, 1:2], v[:, 0:1], 0.5, None, ALU.mult)
                            nc.vector.tensor_scalar(v[:, 2:3].bitcast(I32), v[:, 0:1].bitcast(I32), 1, None,
                                                    ALU.logical_shift_right).then_inc(s_sh2, 1)
                        if k == 6:
                            wait(dve, s_sh2, at.pairs(-3, add=1))
                            nc.vector.tensor_scalar(v[:, 3:4].bitcast(I32), v[:, 2:3].bitcast(I32), -1.0,
                                                    float(0x5F3759DF), ALU.mult, ALU.add).then_inc(s_guess, 1)
                    if k == 6 and at.r % 2 == 0 and at.has(-4):
                        p = at.odd_pair(-4)
                        wait(dve, s_nw, at.pairs(-4, 12, 12))
                        wait(dve, s_xt, at.pairs(-4))
                        wait(dve, s_xcp, at.pairs(-4))
                        apart(dve)
                        nc.vector.tensor_scalar(xs[:], X[:, bass.ds(at.pair(-4), 1), :].rearrange("p a t -> p (a t)"),
                                                mv2[:, p, 0:1], vv[:, p, 3:4], ALU.subtract, ALU.mult).then_inc(s_xs, 1)
                    if k == 2 and at.r % 2 == 0 and at.has(-6):
                        if at.i is None and at.r == 6:
                            dve.wait_ge(s_wr, 32)
                        wait(dve, s_lg, at.pairs(-6, add=1))
                        apart(dve)
                        nc.vector.tensor_tensor(LG[:, bass.ds(E * at.pair(-6), E)], bank_b[:, 0:E],
                                                br[:], ALU.add).then_inc(s_lge, 1)
                    if k == 4 and at.has(6):
                        h = at.mod(2)
                        wait(dve, s_proj, at.value(1, 7))
                        wait(dve, s_p1, at.value(1, 5))
                        nc.vector.scalar_tensor_tensor(rc[:, h, :], bank_b[:, 0:T], bias[:, 2 * h:2 * h + 1],
                                                       tab[:, 0, :], ALU.add, ALU.mult)
                        nc.vector.scalar_tensor_tensor(rs[:, h, :], bank_b[:, T:2 * T], bias[:, 2 * h + 1:2 * h + 2],
                                                       tab[:, 1, :], ALU.add, ALU.mult).then_inc(s_rope, 1)
                    if k == 5 and at.has(-1):
                        o = bank_a[:].rearrange("p (g e) -> p g e", e=32)
                        wait(dve, s_T1, at.value(1, 0))
                        wait(dve, s_On, at.value(1, -1))
                        nc.vector.reciprocal(rden[:], o[:, :, D]).then_inc(s_rc, 1)
                        wait(dve, s_rc, at.value(1, 0))
                        half = at.mod(2, -1)
                        if half == 0:
                            wait(dve, s_BT, at.pairs(-1, add=-1))
                        nc.vector.tensor_tensor(
                            On[at.odd_pair(-1)][:, :, C * half:C * half + C].rearrange("p a (h e) -> p a h e", e=D),
                            o[:, :, 0:D].rearrange("p (a h) e -> p a h e", a=2),
                            rden[:].rearrange("p (a h o) -> p a h o", a=2, o=1).to_broadcast([P, 2, H, D]),
                            ALU.mult).then_inc(s_On, 1)
                if at.i is None and at.r == -4:
                    rest_of_stats()

            steps(dve, step)

            done = [0]

            def then(ins):
                done[0] += 1
                ins.then_inc(s_rt, 1)
                dve.wait_ge(s_rt, done[0])

            def by_expert(t):
                return t[:].rearrange("p (n e) -> p n e", e=E)

            def over_experts(v):
                return v.rearrange("p (n o) -> p n o", o=1).to_broadcast([P, TT, E])

            def over_tiles(v):
                return v.rearrange("p (o e) -> p o e", o=1).to_broadcast([P, TT, E])

            dve.wait_ge(s_wx, 16 * 16)
            dve.wait_ge(s_lge, TT)
            number = over_tiles(cnt[:, 0:E])
            for k, oh in enumerate((OH0, OH1)):
                logits = LG if k == 0 else PA
                then(nc.vector.tensor_reduce(m1[:, k, :], by_expert(logits), AX.X, ALU.max))
                then(nc.vector.tensor_tensor(by_expert(GE), by_expert(logits), over_experts(m1[:, k, :]), ALU.is_ge))
                then(nc.vector.tensor_tensor(by_expert(PB), by_expert(GE), number, ALU.mult))
                then(nc.vector.tensor_reduce(ix[:, k, :], by_expert(PB), AX.X, ALU.min))
                then(nc.vector.tensor_tensor(by_expert(oh), number, over_experts(ix[:, k, :]), ALU.is_equal))
                if k == 0:
                    then(nc.vector.scalar_tensor_tensor(PA[:], OH0[:], -3e38, LG[:], ALU.mult, ALU.add))
            nc.vector.tensor_tensor(MM[:], OH0[:], OH1[:], ALU.add).then_inc(s_mm, 1)
            nc.vector.tensor_tensor(prob[:, 1, :], m1[:, 1, :], m1[:, 0, :], ALU.subtract)
            nc.vector.tensor_tensor(by_expert(PB), by_expert(LG), over_experts(m1[:, 0, :]), ALU.subtract).then_inc(s_ex, 1)
            dve.wait_ge(s_pos, 1)
            then(nc.vector.memset(PA[:, 0:E], 0.0))
            then(nc.vector.tensor_copy(PA[:, E:TT * E], all_bank[:, 0:(TT - 1) * E]))
            a, b = PA, GE
            for d in (1, 2, 4, 8, 16):
                nc.vector.tensor_copy(b[:, 0:d * E], a[:, 0:d * E])
                then(nc.vector.tensor_tensor(b[:, d * E:], a[:, d * E:], a[:, 0:(TT - d) * E], ALU.add))
                a, b = b, a
            then(nc.vector.tensor_tensor(nt[:, 0, :], a[:, (TT - 1) * E:], all_bank[:, (TT - 1) * E:TT * E], ALU.add))
            then(nc.vector.tensor_tensor(b[:].rearrange("p (e n) -> p e n", e=E),
                                         nt[:, 0, :].rearrange("p (e o) -> p e o", o=1).to_broadcast([P, E, TT]),
                                         cnt[:, E:E + TT].rearrange("p (o n) -> p o n", o=1).to_broadcast([P, E, TT]),
                                         ALU.is_gt))
            then(nc.vector.tensor_reduce(nt[:, 1, :], b[:].rearrange("p (e n) -> p e n", e=E), AX.X, ALU.add))
            upto = cnt[:, E + TT + NS:].rearrange("p (e f) -> p e f", e=E)
            then(nc.vector.tensor_tensor(b[:, 0:E * E].rearrange("p (e f) -> p e f", e=E), upto,
                                         nt[:, 1, :].rearrange("p (o f) -> p o f", o=1).to_broadcast([P, E, E]), ALU.mult))
            then(nc.vector.tensor_reduce(nt[:, 2, :], b[:, 0:E * E].rearrange("p (e f) -> p e f", e=E), AX.X, ALU.add))
            then(nc.vector.tensor_tensor(nt[:, 3, :], nt[:, 2, :], nt[:, 1, :], ALU.subtract))
            then(nc.vector.tensor_tensor(a[:], a[:], before_bank[:], ALU.add))
            then(nc.vector.tensor_scalar(nt[:, 3, :], nt[:, 3, :], float(P), None, ALU.mult))
            then(nc.vector.tensor_tensor(by_expert(a), by_expert(a), over_tiles(nt[:, 3, :]), ALU.add))
            for k, oh in enumerate((OH0, OH1)):
                then(nc.vector.tensor_tensor(b[:], a[:], oh[:], ALU.mult))
                then(nc.vector.tensor_reduce(slot_f[:, k, :], by_expert(b), AX.X, ALU.add))
            nc.vector.tensor_copy(slot[:], slot_f[:]).then_inc(s_slot, 1)
            big = xg[0:1].rearrange("p a t -> p (a t)")[:, 0:NS * E].rearrange("p (j e) -> p j e", e=E)
            then(nc.vector.tensor_tensor(big, nt[0:1, 2, :].rearrange("p (o e) -> p o e", o=1).to_broadcast([1, NS, E]),
                                         cnt[0:1, E + TT:E + TT + NS].rearrange("p (j o) -> p j o", o=1)
                                         .to_broadcast([1, NS, E]), ALU.is_le))
            then(nc.vector.tensor_reduce(owner_f[:], big, AX.X, ALU.add))
            then(nc.vector.tensor_scalar(owner_f[:], owner_f[:], float(E - 1), None, ALU.min))
            nc.vector.tensor_copy(owner[:], owner_f[:]).then_inc(s_owner, 1)
            dve.wait_ge(s_ex, 3)
            then(nc.vector.tensor_reduce(prob[:, 2, :], by_expert(PC), AX.X, ALU.add))
            then(nc.vector.reciprocal(prob[:, 3, :], prob[:, 2, :]))
            then(nc.vector.tensor_tensor(prob[:, 1, :], prob[:, 0, :], prob[:, 3, :], ALU.mult))
            then(nc.vector.scalar_tensor_tensor(prob[:, 2, :], prob[:, 3, :], 1e-9, prob[:, 1, :], ALU.add, ALU.add))
            then(nc.vector.reciprocal(prob[:, 0, :], prob[:, 2, :]))
            nc.vector.tensor_tensor(gate[:, 0, :], prob[:, 3, :], prob[:, 0, :], ALU.mult)
            then(nc.vector.tensor_tensor(gate[:, 1, :], prob[:, 1, :], prob[:, 0, :], ALU.mult))

            def product(at, n, base):
                if at.has(-1, n):
                    implied(dve, at, s_h, at.value(1, base - 2))
                    wait(dve, s_si, at.value(1, base))
                    nc.vector.tensor_tensor(ar[at.mod(2, -1)][:], sg[:, at.mod(2, -1), 0:I],
                                            up_bank[at.mod(2, -1)][:, I:2 * I], ALU.mult).then_inc(s_a, 1)

            def shared(at):
                product(at, TT, 0)
                if at.has(-4, TT):
                    wait(dve, s_d, at.value(1, -3))
                    apart(dve)
                    xp = X[:, bass.ds(at.batch(-4), 1), :].rearrange("p a t -> p (a t)")
                    nc.vector.tensor_tensor(xp, xp, down_bank[at.mod(2, -4)][:, 0:T], ALU.add).then_inc(s_ye, 1)

            steps(dve, shared, 0, (6, 32), TT + 4, 2)

            def slot_products(at):
                product(at, NS, TT)
                if at.has(-4, NS):
                    wait(dve, s_d, at.value(1, TT - 3))
                    wait(dve, s_put[at.mod(4)], at.turns(-4, 4, 16))
                    nc.vector.tensor_copy(ys[:, at.mod(4), :], down_bank[at.mod(2)][:, 0:T]).then_inc(s_ye, 1)

            steps(dve, slot_products, 0, (8, 80), NS + 4, 8)

            def combine(at):
                m = at.mod(2)
                wait(dve, s_y[m], at.turns(0, 2, 32, 32))
                apart(dve)
                for n in range(4):
                    for k in range(2):
                        xp = X[:, bass.ds(4 * at.batch() + n, 1), :].rearrange("p a t -> p (a t)")
                        last = nc.vector.scalar_tensor_tensor(
                            xp if k == 1 else half_sum[n], pair_in[:, m, k, n, :],
                            gate[:, k, bass.ds(4 * at.batch() + n, 1)],
                            half_sum[n] if k == 1 else xp, ALU.mult, ALU.add)
                        if k == 0:
                            last.then_inc(s_hs, 1)
                            wait(dve, s_hs, at.value(4, n + 1))
                            apart(dve)
                last.then_inc(s_comb, 1)

            steps(dve, combine, 0, (2, 8), 8, 2)

        @block.tensor
        def _(pe):
            pe.wait_ge(s_wd, 32)
            pe.wait_ge(s_w, 48)
            nc.tensor.matmul(bank_a[:, 0:1], w[:, 5, :], bias[:, 5:6], start=True, stop=True).then_inc(s_bo, 1)
            pe.wait_ge(s_beff, 1)

            def held(at, bank, main):
                for sem_, value, most in ((main,) if at.i is not None else (main, *readers(at, bank))):
                    wait(pe, sem_, value, most)

            def readers(at, bank):
                even = at.r % 2 == 0
                if bank is bank_a:
                    return ((s_tme, at.value(1, 1), NB), (s_On, at.value(1, -1), NB),
                            (s_Ve, at.pairs(0 if even else 1, add=1), NP))
                last, norm = (-4, -8) if even else (-3, -7)
                return ((s_rope, at.value(1, 6), NB), (s_BTe, at.pairs(last, add=1), NP),
                        (s_x2, at.pairs(-4 if even else -5, add=1), NP),
                        (s_xte, at.pairs(norm if even else -7, add=1), NP), (s_lge, at.pairs(norm, add=1), NP))

            def values(at, group, chunk):
                off = -group
                if chunk == 0:
                    wait(pe, s_exp, at.value(8, 8 * off + 4 * group + 4))
                    if group == 0:
                        wait(pe, s_Ve, at.pairs(0, add=1))
                        wait(pe, s_Oe, at.value(1, 0))
                b = at.mod(2, off)
                for j in range(4):
                    h = 4 * group + j
                    last = nc.tensor.matmul(bank_o[32 * j:32 * j + 32, T * group:T * group + T],
                                            V[at.odd_pair(off)][:, chunk, b, h, :],
                                            Pr[h][:, T * chunk:T * chunk + T],
                                            start=(chunk == 0), stop=(chunk == 1))
                if chunk == 1:
                    last.then_inc(s_PV, 1)

            def step(at):
                even = at.r % 2 == 0
                for k in range(H):
                    if at.has(2):
                        c = at.mod(4, 2)
                        if k == 0:
                            v = 32 * ((at.r + 2) // 4 + 1)
                            wait(pe, s_stk[c], v if at.i is None else 32 * at.i + v)
                        wait(pe, s_red, at.value(8, 16 + k + 1 - S_BACK[at.mod(2)][k]))
                        for t in range(2):
                            last = nc.tensor.matmul(bank_s[S_BANK[at.mod(2)][k]][:, T * t:T * t + T],
                                                    Q[c][0:KR, k, P * t:P * t + P], K[c][0:KR, k, :],
                                                    start=True, stop=True)
                        last.then_inc(s_S, 1)
                    if at.has(0):
                        c = at.mod(4)
                        if k == 0:
                            m = at.mod(2)
                            v = 16 * (at.r // 2 + 1)
                            wait(pe, s_mr[m], v if at.i is None else 32 * at.i + v)
                        wait(pe, s_exp, at.value(8, k - 1))
                        for s in range(2):
                            last = nc.tensor.matmul(bank_st[k % 2][:, T * s:T * s + T],
                                                    K[c][0:MROW + 2, k, P * s:P * s + P],
                                                    Q[c][0:MROW + 2, k, :], start=True, stop=True)
                        last.then_inc(s_ST, 1)
                    if not even and k == 0 and at.has(-3):
                        held(at, bank_b, (s_BTe, at.pairs(-3, add=1), NP))
                        nc.tensor.matmul(bank_b[:, 0:T], w[:, 5, :], OT[:], start=True, stop=True).then_inc(s_WO, 1)
                    if even and k == 1 and at.has(-6):
                        if at.i is None and at.r == 6:
                            pe.wait_ge(s_wr, 32)
                        held(at, bank_b, (s_xte, at.pairs(-6, add=1), NP))
                        for c in range(2):
                            last = nc.tensor.matmul(bank_b[:, 0:E], xTs[0][:, c, :], wr[:, c, :],
                                                    start=(c == 0), stop=(c == 1))
                        last.then_inc(s_lg, 1)
                    if k == 2 and at.has(1):
                        wait(pe, s_msp, at.value(1, 2))
                        held(at, bank_a, (s_On, at.value(1, -1), NB) if even else (s_Ve, at.pairs(1, add=1), NP))
                        nc.tensor.transpose(bank_a[:].bitcast(BF16)[0:4 * H, 0:P],
                                            Mb[:, at.mod(2, 1)].rearrange("p a h -> p (a h)"),
                                            ident_b[:]).then_inc(s_TM, 1)
                    if k in (1, 2) and at.has(-1):
                        values(at, 1, k - 1)
                    if k == 3 and at.has(6):
                        p = at.odd_pair(6)
                        if even:
                            wait(pe, s_xn, at.pairs(6, add=1))
                            held(at, bank_b, (s_lge, at.pairs(-6, add=1), NP))
                        else:
                            wait(pe, s_ck[p], at.turns(5, 4, 16, 16))
                            held(at, bank_b, (s_x2, at.pairs(-3, add=1), NP))
                        source = xn if even else ctx_k
                        for r in range(2):
                            last = nc.tensor.matmul(bank_b[:, T * r:T * r + T], w[:, r if even else 2 + r, :],
                                                    source[:, p, :], start=True, stop=True)
                        last.then_inc(s_proj, 1)
                    if k == 4 and at.has(-1):
                        wait(pe, s_Oe, at.value(1, 0))
                        held(at, bank_a, (s_tme, at.value(1, 2), NB))
                        for t in range(2):
                            for g in range(2):
                                col = P * (2 * t + g)
                                last = nc.tensor.transpose(bank_a[:, col:col + P],
                                                           O[:, T * g + P * t:T * g + P * t + P], ident[:])
                        last.then_inc(s_T1, 1)
                    if k in (5, 6) and at.has(0):
                        values(at, 0, k - 5)
                    if even and k == 6 and at.has(-2):
                        wait(pe, s_On, at.value(1, 0))
                        held(at, bank_b, (s_rope, at.value(1, 7), NB))
                        if at.i is None:
                            wait(pe, s_lge, at.pairs(-6, add=1))
                        for t in range(2):
                            last = nc.tensor.transpose(bank_b[:, P * t:P * t + P], On[at.odd_pair(-2)][:, t, :], ident[:])
                        last.then_inc(s_BT, 1)
                    if even and k == 7 and at.has(2):
                        p = at.odd_pair(2)
                        wait(pe, s_cv[p], at.turns(2, 4, 16, 16))
                        held(at, bank_a, (s_On, at.value(1, 0), NB))
                        if at.i is None:
                            wait(pe, s_tme, at.value(1, 2))
                        for s in range(2):
                            last = nc.tensor.matmul(bank_a[:, P * s:P * s + P], ctx_v[:, p, P * s:P * s + P],
                                                    w[:, 4, :], start=True, stop=True)
                        last.then_inc(s_vp, 1)
                    if not even and k == 7 and at.has(-5):
                        wait(pe, s_xs, at.pairs(-5, add=1))
                        held(at, bank_b, (s_rope, at.value(1, 7), NB))
                        if at.i is None:
                            wait(pe, s_x2, at.pairs(-3, add=1), NP)
                        for c in range(2):
                            last = nc.tensor.transpose(bank_b[:, P * c:P * c + P], xs[:, P * c:P * c + P], ident[:])
                        last.then_inc(s_xt, 1)

            pe.wait_ge(s_bo, 2)
            pe.wait_ge(s_zero, 19)
            steps(pe, step)

            pe.wait_ge(s_lge, NP)
            pe.wait_ge(s_x2, NP)
            pe.wait_ge(s_On, NB)
            pe.wait_ge(s_BTe, NP)
            pe.wait_ge(s_red, H * NB)
            pe.wait_ge(s_exp, H * NB)
            pe.wait_ge(s_Oe, NB)
            pe.wait_ge(s_wx, 16 * 16)

            pe.wait_ge(s_mm, 1)
            nc.tensor.matmul(before_bank[:], low[:, 0, :], MM[:], start=True, stop=True)
            nc.tensor.matmul(all_bank[:], low[:, 1, :], MM[:], start=True, stop=True).then_inc(s_pos, 1)

            def tile(at, n, base, load, gate_up, down):
                if at.has(0, n):
                    rows_ = load(at)
                    if at.has(-1, n):
                        wait(pe, s_te, at.value(1, base))
                    for c in range(2):
                        last = nc.tensor.transpose(tile_bank[at.mod(2)][:, P * c:P * c + P],
                                                   rows_[:, P * c:P * c + P], ident[:])
                    last.then_inc(s_t, 1)
                if at.has(-1, n):
                    m = at.mod(2, -1)
                    implied(pe, at, s_te, at.value(1, base))
                    weights = gate_up(at)
                    for c in range(2):
                        last = nc.tensor.matmul(up_bank[m][:, 0:2 * I], xTs[m][:, c, :], weights(c),
                                                start=(c == 0), stop=(c == 1))
                    last.then_inc(s_g, 1)
                if at.has(-2, n):
                    m = at.mod(2, -2)
                    implied(pe, at, s_he, at.value(1, base - 3))
                    wait(pe, s_a, at.value(1, base - 1))
                    nc.tensor.transpose(mid_bank[m][:, 0:P], ar[m][:], ident[:]).then_inc(s_h, 1)
                if at.has(-4, n):
                    m = at.mod(2, -4)
                    implied(pe, at, s_ye, at.value(1, base - 5))
                    implied(pe, at, s_he, at.value(1, base - 3))
                    weights = down(at)
                    nc.tensor.matmul(down_bank[m][:, 0:T], aT[m][:, 0:P], weights,
                                     start=True, stop=True).then_inc(s_d, 1)

            pe.wait_ge(s_slot, 1)

            def row_copy(at):
                wait(pe, s_in, at.value(1, 1))
                return xn[:, at.mod(2), :]

            steps(pe, lambda at: tile(at, TT, 0, row_copy, lambda at: lambda c: sgu[:, c, :], lambda at: sd[:]),
                  0, (6, 32), TT + 4, 2)

            pe.wait_ge(s_owner, 1)
            expert = {}

            def slot_rows(at):
                wait(pe, s_xg[at.mod(8)], at.turns(0, 8, 16, 16))
                return xg[:, at.mod(8), :]

            def slot_gate_up(at):
                e = expert_of(at, -1)
                if at.i is None:
                    apart(pe)
                return lambda c: wgu[:, bass.ds(e, 1), c, :].rearrange("p a i -> p (a i)")

            def slot_down(at):
                key = (at.i is None, at.r - 4)
                e = expert[key] if key in expert else expert_of(at, -4)
                if at.i is None:
                    apart(pe)
                return wd[:, bass.ds(e, 1), :].rearrange("p a t -> p (a t)")

            def expert_of(at, off):
                e = nc.values_load(owner[0:1, bass.ds(at.batch(off), 1)], engines=[mybir.EngineType.PE],
                                   min_val=0, max_val=E - 1,
                                   skip_runtime_bounds_check_because="a count of experts, at most E - 1 by its minimum")
                expert[(at.i is None, at.r + off)] = e
                return e

            steps(pe, lambda at: tile(at, NS, TT, slot_rows, slot_gate_up, slot_down), 0, (8, 80), NS + 4, 8)


def kernel(**inputs):
    import numpy as np
    import concourse.bacc as bacc
    from concourse.bass_utils import run_bass_kernel_spmd as run

    H, D, T = 8, 8, 256
    x = np.ascontiguousarray(np.asarray(inputs["x"]).reshape(4096, T))
    ctx = np.ascontiguousarray(np.asarray(inputs["ctx_2048"]).reshape(4096, T))

    def by_channel(a, turn=0):
        v = np.asarray(a).reshape(H, D, *np.asarray(a).shape[1:])
        return np.roll(v, -turn, axis=1).swapaxes(0, 1).reshape(np.asarray(a).shape)

    g = {n: np.asarray(inputs["L0_xattn_" + n]) for n in ("Wq", "Wk", "Wv", "Wo", "bq", "bk", "bv", "bo")}
    w6 = np.stack([by_channel(g["Wq"]).T, by_channel(g["Wq"], 4).T, by_channel(g["Wk"]).T,
                   by_channel(g["Wk"], 4).T, g["Wv"].T, g["Wo"].T], axis=1)
    b6 = np.stack([by_channel(g["bq"]), by_channel(g["bq"], 4), by_channel(g["bk"]), by_channel(g["bk"], 4),
                   g["bo"], g["bv"]], axis=1)
    freq = (1.0 / np.float32(10000.0) ** (np.arange(0, D, 2, dtype=np.float32) / np.float32(D))).astype(np.float32)
    ang = np.arange(T, dtype=np.float32)[None, :] * np.tile(freq, 2)[:, None]
    sign = np.where(np.arange(D) < D // 2, -1.0, 1.0).astype(np.float32)[:, None]
    one = np.stack([np.cos(ang), np.sin(ang) * sign], axis=1).astype(np.float32)
    rope = np.tile(np.repeat(one, H, axis=0), (2, 1, 1))

    arrays = {"x_dram": x, "ctx_dram": ctx, "w6": np.ascontiguousarray(w6),
              "bias6": np.ascontiguousarray(np.tile(b6, (2, 1))), "rope": np.ascontiguousarray(rope),
              "ident_dram": np.eye(128, dtype=np.float32)}
    m = {n: np.asarray(inputs["L0_ffn_" + n]) for n in ("Wr", "bias", "Wg", "Wu", "Wd", "sWg", "sWu", "sWd")}
    E, P = 16, 128
    counts = np.concatenate([np.arange(E) - 1024.0, np.arange(32) * 128.0, np.arange(80),
                             np.tril(np.ones((E, E))).reshape(-1)]).astype(np.float32)
    below = np.stack([np.triu(np.ones((P, P)), 1), np.ones((P, P))], axis=1).astype(np.float32)
    arrays |= {
        "w_router": np.ascontiguousarray(m["Wr"].T), "b_router": np.tile(m["bias"][None], (P, 1)),
        "w_gu": np.concatenate([m["Wg"], m["Wu"]], axis=2), "w_down": np.ascontiguousarray(m["Wd"]),
        "s_gu": np.concatenate([m["sWg"], m["sWu"]], axis=1), "s_down": np.ascontiguousarray(m["sWd"]),
        "counts": np.tile(counts, (P, 1)), "below": below,
    }
    nc = bacc.Bacc("TRN2", target_bir_lowering=False, num_devices=1)
    args = [nc.dram_tensor(n, a.shape, mybir.dt.from_np(a.dtype), kind="ExternalInput").ap() for n, a in arrays.items()]
    out = nc.dram_tensor("out", (4096, T), F32, kind="ExternalOutput").ap()
    xattn_moe(nc, *args, out)
    r = run(nc, [arrays], core_ids=[0])
    return r.results[0]["out"].reshape(64, 64, T)
```

```python
from contextlib import ExitStack

import concourse.bass as bass
from concourse import mybir

ALU = mybir.AluOpType
ACT = mybir.ActivationFunctionType
AX = mybir.AxisListType
F32 = mybir.dt.float32
BF16 = mybir.dt.bfloat16
I32 = mybir.dt.int32


class Step:

    def __init__(self, r, i=None, turn=4):
        self.r, self.i, self.turn = r, i, turn

    def batch(self, off=0):
        return self.r + off if self.i is None else self.turn * self.i + (self.r + off)

    def pair(self, off=0):
        h = (self.r + off) // 2
        return h if self.i is None else self.turn // 2 * self.i + h

    def mod(self, n, off=0):
        return (self.r + off) % n

    def odd_pair(self, off=0):
        return (self.r + off) // 2 % 2

    def value(self, per_batch, add):
        v = per_batch * self.r + add
        return v if self.i is None else (self.turn * per_batch) * self.i + v

    def pairs(self, off, per=1, add=0):
        v = per * ((self.r + off) // 2) + add
        return v if self.i is None else (self.turn // 2 * per) * self.i + v

    def turns(self, off, n, per, add=0):
        v = per * ((self.r + off) // n) + add
        return v if self.i is None else (self.turn // n * per) * self.i + v

    def has(self, off, n=64):
        return self.i is not None or 0 <= self.r + off < n


def wait(eng, sem, value, most=None):
    if isinstance(value, int):
        if most is not None:
            value = min(value, most)
        if value <= 0:
            return
    eng.wait_ge(sem, value)


def xattn_moe(nc, x, ctx_in, w6, bias6, rope, ident_in, w_router, b_router, w_gu, w_down,
              shared_gu, shared_down, counts, below, out):
    NB, C, T = 64, 64, 256
    P = 128
    H, D = 8, 8
    NP = NB // 2
    PARTS = 3
    KR = PARTS * PARTS * D
    MROW = 96
    SCALE = float(D) ** -0.5
    EPS = 1e-5
    E, I = 16, 128
    TT = NP
    NS = 80
    ROW = T + 4
    BIG = 1024.0

    slots = nc.dram_tensor("slots", (NS * P, ROW), F32, kind="Internal").ap()
    results = nc.dram_tensor("results", (2 * TT * P, T), F32, kind="Internal").ap()
    SLOTS = PARTS + 2 * PARTS - 1
    scratch = nc.dram_tensor("parts", (NB, SLOTS, C, T), BF16, kind="Internal").ap()

    with ExitStack() as stack:
        def sb(name, shape, dt=F32):
            return stack.enter_context(nc.sbuf_tensor(name, shape, dt))

        def psum(name):
            return stack.enter_context(nc.psum_tensor(name, [P, 512], F32))

        def sem(name):
            return stack.enter_context(nc.semaphore(name))

        X = sb("X", [P, NP, T])
        ctx_kv = sb("ctx_kv", [P, 4, T])
        ctx_k, ctx_v = ctx_kv[:, 0:2], ctx_kv[:, 2:4]
        w = sb("w", [P, 6, P])
        bias = sb("bias", [P, 6])
        beff = sb("beff", [P, 1])
        tab = sb("tab", [P, 2, T])
        ident = sb("ident", [P, P])
        ident_b = sb("ident_b", [P, P], BF16)
        eps = sb("eps", [P, 1])
        st1 = sb("st1", [P, 2, 6])
        mv1 = sb("mv1", [P, NP, 2])
        std1 = sb("std1", [P, NP])
        rstd1 = sb("rstd1", [P, NP])
        shift1 = sb("shift1", [P, NP])
        xn = sb("xn", [P, 2, T])
        work = sb("work", [P, 4, 2, T])
        rc, rs, qk, rest = [work[:, i] for i in range(4)]
        parts_sb = sb("parts_sb", [P, 2 * 2 * PARTS * T], BF16)
        parts = parts_sb[:].rearrange("p (n s k t) -> p n s k t", n=2, s=2, k=PARTS)
        QK = sb("QK", [P, 8, H, T], BF16)
        Q = [QK[:, i] for i in range(4)]
        K = [QK[:, 4 + i] for i in range(4)]
        M = sb("M", [P, 2, 2 * H])
        Mb = sb("Mb", [P, 2, 2, 2 * H], BF16)
        Mt = sb("Mt", [4 * H, 2, P], BF16)
        wide = sb("wide", [P, 8 * ROW])
        V = [wide[:, 1024 * i:1024 * i + 1024].rearrange("p (s b h e) -> p s b h e", s=2, b=2, h=H) for i in range(2)]
        Pr = [sb(f"Pr{i}", [P, 2 * T]) for i in range(H)]
        O = sb("O", [P, 2 * T])
        rden = sb("rden", [P, 16])
        On = [sb(f"On{i}", [P, 2, P]) for i in range(2)]
        OT = sb("OT", [P, T])
        st2 = sb("st2", [P, 6])
        mv2 = sb("mv2", [P, 2, 2])
        vv = sb("vv", [P, 2, 4])
        newton = sb("newton", [P, 3])

        rows = sb("rows", [P, TT, ROW])
        xT_sb = sb("xT_sb", [P, 2 * T + 4])
        xTs = [xT_sb[:, T * i:T * i + T].rearrange("p (c n) -> p c n", c=2) for i in range(2)]
        blank = xT_sb[:, T:T + ROW]
        xs = sb("xs", [P, T])
        wr = sb("wr", [P, 2, E])
        wgu = sb("wgu", [P, E, 2, 2 * I])
        wd = sb("wd", [P, E, T])
        late = parts_sb[:].bitcast(F32)
        sgu = late[:, 0:512].rearrange("p (c i) -> p c i", c=2)
        sd = late[:, 512:768]
        cnt = late[:, 768:1152]
        low = late[:, 1152:1408].rearrange("p (a n) -> p a n", a=2)
        br = sb("br", [P, E])
        LG = sb("LG", [P, TT * E])
        GE, OH0, OH1, MM, PA, PB, PC = [Pr[i] for i in range(7)]
        slot = sb("slot", [P, 2, TT], mybir.dt.int32)
        prob = On[0][:, 0, :].rearrange("p (k n) -> p k n", n=TT)
        nt = On[0][:, 1, 0:4 * E].rearrange("p (k e) -> p k e", e=E)
        slot_f = On[0][:, 1, 4 * E:4 * E + 2 * TT].rearrange("p (k n) -> p k n", n=TT)
        fresh = O
        m1, ix = [On[1][:, 0, 2 * TT * i:2 * TT * i + 2 * TT].rearrange("p (k n) -> p k n", n=TT) for i in range(2)]
        gate = On[1][:, 1, 0:2 * TT].rearrange("p (k n) -> p k n", n=TT)
        owner_f = sb("owner_f", [1, NS])
        owner = sb("owner", [1, NS], mybir.dt.int32)
        ids_out = sb("ids_out", [P, 8], mybir.dt.int32)
        xg = wide[:].rearrange("p (a t) -> p a t", a=8)
        sg = work[:, 0:2].rearrange("p a b t -> p a (b t)")
        aT = [work[:, 2 + i].rearrange("p b t -> p (b t)") for i in range(2)]
        ar = [OT[:, P * i:P * i + P] for i in range(2)]
        late_qk = QK[:].bitcast(F32).rearrange("p a h t -> p (a h t)")
        ys = late_qk[:, 0:8 * T].rearrange("p (a t) -> p a t", a=8)
        pair_in = late_qk.rearrange("p (m k n t) -> p m k n t", m=4, k=2, n=4)
        half_sum = [Pr[4 + n // 2][:, T * (n % 2):T * (n % 2) + T] for n in range(8)]

        bank_s = [psum(f"bank_s{i}") for i in range(3)]
        bank_st = [psum(f"bank_st{i}") for i in range(2)]
        bank_o = psum("bank_o")
        bank_a = psum("bank_a")
        bank_b = psum("bank_b")
        tile_bank = (bank_a, bank_b)
        before_bank, all_bank = bank_s[0:2]
        EARLY = 30
        up_bank, mid_bank, down_bank = bank_st, (bank_o, bank_s[2]), bank_s[0:2]
        taken = [((n - 11) % 16 % 3, 1)[(n - 11) % 16 == 15] for n in range(2 * H)]
        S_BANK = (taken[:H], taken[H:])
        S_BACK = [[next(d for d in range(1, 9) if taken[H * m + k - d] == taken[H * m + k]) for k in range(H)]
                  for m in range(2)]

        s_x = [sem(f"s_xin{g}") for g in range(8)]
        s_w = sem("s_w")
        s_zero = sem("s_zero")
        s_pad = sem("s_pad")
        s_padc = sem("s_padc")
        s_wd = sem("s_wd")
        s_ck = [sem(f"s_ck{i}") for i in range(2)]
        s_cv = [sem(f"s_cv{i}") for i in range(2)]
        s_ptw = [sem(f"s_ptw{i}") for i in range(4)]
        s_stk = [sem(f"s_stk{i}") for i in range(4)]
        s_mr = [sem(f"s_mr{i}") for i in range(2)]
        s_st1 = sem("s_st1")
        s_mv1 = sem("s_mv1")
        s_std1 = sem("s_std1")
        s_rstd1 = sem("s_rstd1")
        s_rc1 = sem("s_rc1")
        s_xn = sem("s_xn")
        s_proj = sem("s_proj")
        s_vp = sem("s_vp")
        s_rope = sem("s_rope")
        s_qk = sem("s_qk")
        s_p1 = sem("s_p1")
        s_r1 = sem("s_r1")
        s_p2 = sem("s_p2")
        s_pt = sem("s_pt")
        s_S = sem("s_S")
        s_red = sem("s_red")
        s_hi = sem("s_hi")
        s_msp = sem("s_msp")
        s_TM = sem("s_TM")
        s_tme = sem("s_tme")
        s_ST = sem("s_ST")
        s_exp = sem("s_exp")
        s_PV = sem("s_PV")
        s_Ve = sem("s_Ve")
        s_Oe = sem("s_Oe")
        s_T1 = sem("s_T1")
        s_rc = sem("s_rc")
        s_On = sem("s_On")
        s_BT = sem("s_BT")
        s_BTe = sem("s_BTe")
        s_WO = sem("s_WO")
        s_x2 = sem("s_x2")
        s_st2 = sem("s_st2")
        s_guess = sem("s_guess")
        s_nw = sem("s_nw")
        s_vv = sem("s_vv")
        s_sh2 = sem("s_sh2")
        s_mv2 = sem("s_mv2")
        s_bo = sem("s_bo")
        s_beff = sem("s_beff")
        s_wx = sem("s_wx")
        s_wr = sem("s_wr")
        s_blank = sem("s_blank")
        s_fill = sem("s_fill")
        s_id = sem("s_id")
        s_xs = sem("s_xs")
        s_xcp = sem("s_xcp")
        s_xt = sem("s_xt")
        s_xte = sem("s_xte")
        s_lg = sem("s_lg")
        s_lge = sem("s_lge")
        s_mm = sem("s_mm")
        s_pos = sem("s_pos")
        s_ex = sem("s_ex")
        s_rt = sem("s_rt")
        s_slot = sem("s_slot")
        s_first = [sem(f"s_first{i}") for i in range(2)]
        s_owner = sem("s_owner")
        s_in = sem("s_in")
        s_t = sem("s_t")
        s_te = sem("s_te")
        s_g = sem("s_g")
        s_si = sem("s_si")
        s_a = sem("s_a")
        s_h = sem("s_h")
        s_he = sem("s_he")
        s_d = sem("s_d")
        s_ye = sem("s_ye")
        s_comb = sem("s_comb")
        s_hs = sem("s_hs")
        s_second = sem("s_second")
        s_xg = [sem(f"s_xg{i}") for i in range(8)]
        s_put = [sem(f"s_put{i}") for i in range(8)]
        s_idc = sem("s_idc")
        s_y = [sem(f"s_y{i}") for i in range(4)]
        s_o = [sem(f"s_o{i}") for i in range(2)]

        FIRST, LAST = -8, 69
        LOOP = (8, 56)

        def steps(eng, step, first=FIRST, loop=LOOP, last=LAST, turn=4):
            for b in range(first, loop[0]):
                step(Step(b, None, turn))
            with eng.Fori(loop[0] // turn, loop[1] // turn) as i:
                for r in range(turn):
                    step(Step(r, i, turn))
            for b in range(loop[1], last):
                step(Step(b, None, turn))

        def implied(eng, at, sem_, value):
            if at.i is None:
                wait(eng, sem_, value)


        PAD = 64
        MINUS = -1.0058441162109375
        Qf, Kf = [q.bitcast(F32) for q in Q], [k.bitcast(F32) for k in K]

        def apart(eng):
            eng.wait_ge(s_w, 48)

        block = stack.enter_context(nc.Block())

        @block.sync
        def _(sp):
            def load_x(g):
                sp.dma_start(X[:, 4 * g:4 * g + 4, :],
                             x.rearrange("(n p) t -> p n t", p=P)[:, 4 * g:4 * g + 4, :]).then_inc(s_x[g], 16)

            load_x(0)
            sp.dma_start(bias[:], bias6).then_inc(s_w, 16)
            sp.dma_start(tab[:], rope).then_inc(s_w, 16)
            sp.dma_start(ident[:], ident_in).then_inc(s_w, 16)
            sp.wait_ge(s_zero, 1)
            sp.dma_start(w[0:C, :, 0:C], w6).then_inc(s_wd, 16)
            sp.dma_start(w[C:P, :, C:P], w6).then_inc(s_wd, 16)

            def alone(sem_, value):
                wait(sp, sem_, known(value))

            def known(index):
                if not isinstance(index, int):
                    sp.compute_val(index)
                return index

            def load(dst, sems, at, off, pair):
                p = at.odd_pair(off)
                sp.dma_start(dst[:, p:p + 1, :].rearrange("p a t -> p (a t)"),
                             ctx_in.rearrange("(n p) t -> n p t", p=P)[bass.ds(pair, 1), :, :]
                             .rearrange("n p t -> (n p) t")).then_inc(sems[p], 16)

            def weights(n):
                e = 4 * n
                if n == 0:
                    sp.dma_start(wr[:], w_router.rearrange("(c p) i -> p c i", p=P)).then_inc(s_wr, 16)
                    sp.dma_start(br[:], b_router).then_inc(s_wr, 16)
                for c in range(2):
                    sp.dma_start(wgu[:, e:e + 4, c, :],
                                 w_gu.rearrange("e (c p) i -> p e c i", p=P)[:, e:e + 4, c, :]).then_inc(s_wx, 16)
                sp.dma_start(wd[:, e:e + 4, :], w_down[e:e + 4].rearrange("e p t -> p e t")).then_inc(s_wx, 16)

            def late_weights():
                for n in range(4):
                    sp.wait_ge(s_ptw[n], (32, 64)[n % 2] * NP // 2)
                sp.dma_start(sgu, shared_gu.rearrange("(c p) i -> p c i", p=P)).then_inc(s_wx, 16)
                for dst, src in ((sd, shared_down), (cnt, counts), (low, below)):
                    sp.dma_start(dst, src).then_inc(s_wx, 16)

            def fill(n):
                alone(s_blank, 2)
                sp.dma_start(slots.rearrange("(n p) t -> p n t", p=P)[:, 10 * n:10 * n + 10, :],
                             blank.rearrange("p (o t) -> p o t", o=1).to_broadcast([P, 10, ROW])).then_inc(s_fill, 16)

            def step(at):
                if at.i is None and at.r == -7:
                    for g in range(1, 8):
                        load_x(g)
                if at.i is None and 0 <= at.r < 4:
                    weights(at.r)
                if at.i is None and 56 <= at.r < 64:
                    fill(at.r - 56)
                if at.i is None and at.r == 62:
                    late_weights()
                if at.r % 2 == 0 and at.has(8):
                    pair = known(at.pair(8))
                    alone(s_proj, at.value(1, 6))
                    load(ctx_k, s_ck, at, 8, pair)
                if at.r % 2 == 0 and at.has(4):
                    pair = known(at.pair(4))
                    alone(s_vp, at.pairs(4, add=-1))
                    load(ctx_v, s_cv, at, 4, pair)
                if at.i is None and at.r == -3:
                    sp.wait_ge(s_pad, 3)
                    sp.wait_ge(s_padc, 6)
                if at.has(3):
                    batch = known(at.batch(3))
                    c = at.mod(4, 3)
                    q_written, k_written = known(at.turns(3, 4, 32, 32)), known(at.turns(3, 4, 64, 64))
                    used = known(at.value(8, 0))
                    alone(s_ptw[2 * at.odd_pair(3)], q_written)
                    alone(s_ptw[2 * at.odd_pair(3) + 1], k_written)
                    alone(s_ST, used)
                    src = scratch[bass.ds(batch, 1)].rearrange("a s c t -> (a s) (c t)")
                    for dst, slot, turn in ((Q[c], 0, 0), (K[c], PARTS, C * T)):
                        g = src[slot:slot + 1]
                        rows = [[turn, PARTS], [H * T, PARTS * D], [1, H * T]]
                        sp.dma_start(dst[0:KR].rearrange("r h t -> r (h t)"),
                                     bass.AP(tensor=g.tensor, offset=g.offset, ap=rows)).then_inc(s_stk[c], 16)
                if at.has(1):
                    alone(s_tme, at.value(1, 2))
                    c = at.mod(4, 1)
                    m = at.mod(2, 1)
                    sp.dma_start(Q[c][MROW:MROW + 2].rearrange("r h t -> r (h t)"), Mt[:, m, :]).then_inc(s_mr[m], 16)
                if at.has(5):
                    pair = known(at.pair(5))
                    alone(s_pt, at.value(1, 6))
                    n, qk_ = at.mod(4, 5), at.mod(2, 5)
                    dst = scratch.rearrange("(n b) s c t -> n b c s t", b=2)
                    for half in range(2):
                        to = dst[bass.ds(pair, 1), half:half + 1].rearrange("n b c s t -> (n b c) s t")
                        own = parts[C * half:C * half + C, at.odd_pair(5), qk_]
                        sp.dma_start(to[:, PARTS * qk_:PARTS * qk_ + PARTS], own).then_inc(s_ptw[n], 16)
                        if qk_:
                            sp.dma_start(to[:, 2 * PARTS:SLOTS], own[:, 0:PARTS - 1, :]).then_inc(s_ptw[n], 16)

            steps(sp, step)

            def feed(at):
                if at.has(0, NS):
                    tile, read = known(at.batch()), known(at.value(1, -7))
                    alone(s_idc, read)
                    sp.dma_start(xg[:, at.mod(8), :],
                                 slots.rearrange("(n p) t -> n p t", p=P)[bass.ds(tile, 1)]
                                 .rearrange("n p t -> (n p) t")).then_inc(s_xg[at.mod(8)], 16)

            sp.wait_ge(s_second, 16 * TT)
            sp.wait_ge(s_owner, 1)
            steps(sp, feed, 0, (8, 72), NS, 8)

            for i in range(8):
                sp.wait_ge(s_put[i], 16 * (NS // 8))
            res = results[0:2 * TT * P].rearrange("(k g n p) t -> p g k n t", k=2, n=4, p=P)

            def gather(at):
                alone(s_comb, at.value(4, 0))
                if at.has(3, TT // 4):
                    g, m = known(at.batch(3)), at.mod(4, 3)
                    for k in range(2):
                        sp.dma_start(pair_in[:, m, k], res[:, bass.ds(g, 1), k]
                                     .rearrange("p g n t -> p (g n) t")).then_inc(s_y[m], 16)
                if at.has(-1, TT // 4):
                    g = known(at.batch(-1))
                    sp.dma_start(out.rearrange("(g n p) t -> p g n t", n=4, p=P)[:, bass.ds(g, 1)]
                                 .rearrange("p g n t -> p (g n) t"),
                                 X[:, bass.ds(4 * g, 4), :]).then_inc(s_o[at.mod(2, -1)], 16)

            for g in range(-3, TT // 4 + 1):
                gather(Step(g))
            for i in range(2):
                sp.wait_ge(s_o[i], 16 * 4)

        @block.gpsimd
        def _(pool):
            pieces = [(w[:], 0.0)]
            for i in range(2):
                pieces += [(V[i][:, :, :, :, 0:8], 0.0), (V[i][:, :, :, :, 9:32], 0.0), (V[i][:, :, :, :, 8:9], 1.0)]
            for n, (piece, fill) in enumerate(pieces):
                wait(pool, s_zero, n)
                nc.gpsimd.memset(piece, fill).then_inc(s_zero, 1)
            pool.wait_ge(s_zero, len(pieces))
            nc.gpsimd.memset(blank, 0.0).then_inc(s_blank, 1)
            pool.wait_ge(s_blank, 1)
            nc.gpsimd.iota(blank[:, T:T + 1].bitcast(mybir.dt.int32), pattern=[[0, 1]], base=2 * TT * P,
                           channel_multiplier=1).then_inc(s_blank, 1)
            pool.wait_ge(s_blank, 2)

            def step(at):
                if at.r % 2 == 0 and at.has(-4):
                    p = at.odd_pair(-4)
                    half, y, t = vv[:, p, 1:2], vv[:, p, 3:4], newton[:, 0:1]
                    wait(pool, s_guess, at.pairs(-4, add=1))
                    n = 0
                    for _ in range(3):
                        for dst, a, b, op in ((t, y, y, ALU.mult), (t, t, half, ALU.mult),
                                              (t, newton[:, 1:2], t, ALU.subtract), (y, y, t, ALU.mult)):
                            wait(pool, s_nw, at.pairs(-4, 14, n))
                            nc.gpsimd.tensor_tensor(dst, a, b, op).then_inc(s_nw, 1)
                            n += 1
                    wait(pool, s_nw, at.pairs(-4, 14, n))
                    nc.gpsimd.tensor_tensor(t, mv2[:, p, 0:1], y, ALU.mult).then_inc(s_nw, 1)
                    wait(pool, s_nw, at.pairs(-4, 14, n + 1))
                    nc.gpsimd.tensor_tensor(vv[:, p, 0:1], newton[:, 2:3], t, ALU.subtract).then_inc(s_nw, 1)
                if at.has(6):
                    p, h = at.odd_pair(6), at.mod(2)
                    wait(pool, s_rope, at.value(1, 7))
                    wait(pool, s_pt, at.value(1, 5))
                    nc.gpsimd.tensor_tensor(qk[:, h], rc[:, h], rs[:, h], ALU.add).then_inc(s_qk, 1)
                    wait(pool, s_ptw[at.mod(4, 6)], at.turns(6, 4, 64 if h else 32))
                    nc.gpsimd.tensor_tensor(parts[:, p, h, 0, :], rc[:, h], rs[:, h], ALU.add).then_inc(s_p1, 1)
                    wait(pool, s_p1, at.value(1, 7))
                    nc.gpsimd.tensor_tensor(rest[:, h], qk[:, h], parts[:, p, h, 0, :], ALU.subtract).then_inc(s_r1, 1)
                    nc.gpsimd.tensor_tensor(parts[:, p, h, 1, :], qk[:, h], parts[:, p, h, 0, :],
                                            ALU.subtract).then_inc(s_p2, 1)
                    wait(pool, s_p2, at.value(1, 7))
                    nc.gpsimd.tensor_tensor(parts[:, p, h, 2, :], rest[:, h], parts[:, p, h, 1, :],
                                            ALU.subtract).then_inc(s_pt, 1)
            steps(pool, step)

            ids = rows[:, :, T:T + 1].bitcast(mybir.dt.int32)
            nc.gpsimd.iota(ids, pattern=[[P, TT], [0, 1]], base=0, channel_multiplier=1).then_inc(s_id, 1)
            nc.gpsimd.memset(rows[:, :, T + 1:ROW], 0.0).then_inc(s_id, 1)

            pool.wait_ge(s_slot, 1)
            pool.wait_ge(s_id, 2)
            pool.wait_ge(s_fill, 16 * 8)
            def scatter(k, half, done):
                for n in range(TT // 2 * half, TT // 2 * (half + 1)):
                    pool.indirect_dma_start(
                        out=slots, out_offset=bass.IndirectOffsetOnAxis(ap=slot[:, k, n:n + 1], axis=0),
                        in_=rows[:, n, :], in_offset=None).then_inc(done, 16)

            for half in range(2):
                scatter(0, half, s_first[half])
            pool.wait_ge(s_slot, 2)
            for half in range(2):
                pool.wait_ge(s_first[half], 16 * TT // 2)
                nc.gpsimd.iota(ids[:, TT // 2 * half:TT // 2 * (half + 1)], pattern=[[P, TT // 2], [0, 1]],
                               base=TT * P + TT // 2 * P * half, channel_multiplier=1).then_inc(s_id, 1)
                pool.wait_ge(s_id, 3 + half)
                scatter(1, half, s_second)

            def put(at):
                if at.has(-4, NS):
                    if at.i is not None:
                        pool.compute_val(at.value(1, TT - 3))
                    apart(pool)
                    wait(pool, s_ye, at.value(1, TT - 3))
                    pool.indirect_dma_start(
                        out=results, out_offset=bass.IndirectOffsetOnAxis(
                            ap=ids_out[:, at.mod(8, -4):at.mod(8, -4) + 1], axis=0),
                        in_=ys[:, at.mod(8, -4), :], in_offset=None,
                        bounds_check=2 * TT * P - 1, oob_is_err=False).then_inc(s_put[at.mod(8, -4)], 16)

            steps(pool, put, 0, (8, 80), NS + 4, 8)

        @block.scalar
        def _(act):
            act.wait_ge(s_mv1, 4)
            nc.scalar.activation(std1[:, 0:4], mv1[:, 0:4, 1], ACT.Sqrt, bias=eps[:, 0:1]).then_inc(s_std1, 1)

            def step(at):
                if at.i is None and at.r == -5:
                    act.wait_ge(s_pad, 3)
                    for i in range(1, 4):
                        nc.scalar.activation(Qf[i][PAD:P], Qf[0][PAD:P], ACT.Copy).then_inc(s_padc, 1)
                        nc.scalar.activation(Kf[i][PAD:P], Kf[0][PAD:P], ACT.Copy).then_inc(s_padc, 1)
                if at.i is None and at.r == -2:
                    act.wait_ge(s_mv1, NP)
                    nc.scalar.activation(std1[:, 4:NP], mv1[:, 4:NP, 1], ACT.Sqrt, bias=eps[:, 0:1]).then_inc(s_std1, 1)
                for k in range(H):
                    if at.has(0):
                        wait(act, s_ST, at.value(8, k + 1))
                        if k % 4 == 0:
                            wait(act, s_PV, at.value(2, -1 + k // 4))
                        nc.scalar.activation(Pr[k][:], bank_st[k % 2][:], ACT.Exp, scale=SCALE).then_inc(s_exp, 1)
                    if k == 1 and at.r % 2 == 0 and at.has(6):
                        p, pair = at.odd_pair(6), at.pair(6)
                        act.wait_ge(s_rstd1, 1 if at.i is None and pair < 4 else 2)
                        wait(act, s_proj, at.value(1, 3))
                        apart(act)
                        nc.scalar.activation(xn[:, p, :], X[:, bass.ds(pair, 1), :].rearrange("p a t -> p (a t)"),
                                             ACT.Identity, scale=rstd1[:, bass.ds(pair, 1)],
                                             bias=shift1[:, bass.ds(pair, 1)]).then_inc(s_xn, 1)
                    if k == 6 and at.r % 2 == 0 and at.has(-4):
                        p = at.odd_pair(-4)
                        wait(act, s_nw, at.pairs(-4, 14, 14))
                        wait(act, s_xt, at.pairs(-4))
                        wait(act, s_xcp, at.pairs(-4))
                        apart(act)
                        nc.scalar.activation(xs[:], X[:, bass.ds(at.pair(-4), 1), :].rearrange("p a t -> p (a t)"),
                                             ACT.Identity, scale=vv[:, p, 3:4], bias=vv[:, p, 0:1]).then_inc(s_xs, 1)
                    if k == 2 and at.has(1):
                        m = at.mod(2, 1)
                        wait(act, s_TM, at.value(1, 2))
                        wait(act, s_mr[m], at.turns(1, 2, 16))
                        nc.scalar.activation(Mt[:, m, :], bank_a[:].bitcast(BF16)[0:4 * H, 0:P], ACT.Copy).then_inc(s_tme, 1)
                    if k == 2 and at.has(-1):
                        wait(act, s_PV, at.value(2, 0))
                        wait(act, s_T1, at.value(1, -1))
                        nc.scalar.activation(O[:], bank_o[:], ACT.Copy).then_inc(s_Oe, 1)
                    if k == 0 and at.r % 2 == 1 and at.has(1):
                        wait(act, s_vp, at.pairs(1, add=1))
                        wait(act, s_PV, at.pairs(1, 4, -4))
                        nc.scalar.activation(
                            V[at.odd_pair(1)][:].rearrange("p s b h e -> p (s b h) e")[:, :, 0:D],
                            bank_a[:].rearrange("p (g e) -> p g e", e=D)[:, 0:32, :], ACT.Copy).then_inc(s_Ve, 1)
                    if k == 7 and at.r % 2 == 0 and at.has(-2):
                        wait(act, s_BT, at.pairs(-2, add=1))
                        wait(act, s_WO, at.pairs(-2))
                        nc.scalar.activation(OT[:], bank_b[:, 0:T], ACT.Copy).then_inc(s_BTe, 1)
                    if k == 3 and at.r % 2 == 1 and at.has(-5):
                        wait(act, s_xs, at.pairs(-5, add=1))
                        apart(act)
                        nc.scalar.activation(rows[:, bass.ds(at.pair(-5), 1), 0:T].rearrange("p a t -> p (a t)"),
                                             xs[:], ACT.Copy).then_inc(s_xcp, 1)
                    if k == 0 and at.r % 2 == 0 and at.has(-6):
                        wait(act, s_xt, at.pairs(-6, add=1))
                        wait(act, s_lg, at.pairs(-6))
                        nc.scalar.activation(xTs[0][:], bank_b[:, 0:2 * P].rearrange("p (c n) -> p c n", c=2),
                                             ACT.Copy).then_inc(s_xte, 1)

            steps(act, step)

            act.wait_ge(s_ex, 1)
            nc.scalar.activation(PC[:], PB[:], ACT.Exp).then_inc(s_ex, 1)
            nc.scalar.activation(prob[:, 0, :], prob[:, 1, :], ACT.Exp).then_inc(s_ex, 1)

            def tile(at, n, base):
                if at.has(0, n):
                    implied(act, at, s_g, at.value(1, base - 1))
                    wait(act, s_t, at.value(1, base + 1))
                    nc.scalar.activation(xTs[at.mod(2)][:], tile_bank[at.mod(2)][:, 0:2 * P]
                                         .rearrange("p (c n) -> p c n", c=2), ACT.Copy).then_inc(s_te, 1)
                if at.has(-3, n):
                    implied(act, at, s_d, at.value(1, base - 4))
                    wait(act, s_h, at.value(1, base - 2))
                    nc.scalar.activation(aT[at.mod(2, -3)][:, 0:P], mid_bank[at.mod(2, -3)][:, 0:P],
                                         ACT.Copy).then_inc(s_he, 1)
                if at.has(-1, n):
                    implied(act, at, s_a, at.value(1, base - 2))
                    wait(act, s_g, at.value(1, base))
                    nc.scalar.activation(sg[:, at.mod(2, -1), 0:I], up_bank[at.mod(2, -1)][:, 0:I],
                                         ACT.Silu).then_inc(s_si, 1)

            def shared(at):
                tile(at, TT, 0)
                if at.has(1, TT):
                    wait(act, s_t, at.value(1, 0))
                    apart(act)
                    nc.scalar.activation(xn[:, at.mod(2, 1), :], rows[:, bass.ds(at.batch(1), 1), 0:T]
                                         .rearrange("p a t -> p (a t)"), ACT.Copy).then_inc(s_in, 1)

            act.wait_ge(s_xcp, NP)
            act.wait_ge(s_fill, 16 * 8)
            steps(act, shared, -1, (6, 30), TT + 3, 2)
            steps(act, lambda at: tile(at, NS, TT), 0, (8, 80), NS + 3, 8)

        @block.vector
        def _(dve):
            nc.vector.memset(eps[:], EPS)
            nc.vector.memset(newton[:, 1:2], 1.5)
            nc.vector.memset(newton[:, 2:3], 0.0)
            for piece, fill in ((Qf[0][PAD:P], 0.0), (Kf[0][PAD:MROW], 0.0), (Kf[0][MROW:P], MINUS)):
                nc.vector.memset(piece, fill).then_inc(s_pad, 1)

            def stats(first, end):
                for p in range(first, end + 1):
                    if p < end:
                        if p % 4 == 0 or p == first:
                            dve.wait_ge(s_x[p // 4], 16)
                        wait(dve, s_mv1, p - 1)
                        nc.vector.bn_stats(st1[:, p % 2, :], X[:, p, :]).then_inc(s_st1, 1)
                    if p > first:
                        dve.wait_ge(s_st1, p)
                        nc.vector.bn_aggr(mv1[:, p - 1, :], st1[:, (p - 1) % 2, :]).then_inc(s_mv1, 1)

            def scales(first, end):
                dve.wait_ge(s_std1, 1 if first == 0 else 2)
                nc.vector.reciprocal(rstd1[:, first:end], std1[:, first:end]).then_inc(s_rc1, 1)
                dve.wait_ge(s_rc1, 1 if first == 0 else 2)
                nc.vector.scalar_tensor_tensor(shift1[:, first:end], mv1[:, first:end, 0], -1.0,
                                               rstd1[:, first:end], ALU.mult, ALU.mult).then_inc(s_rstd1, 1)

            stats(0, 4)
            dve.wait_ge(s_w, 48)
            nc.vector.tensor_copy(ident_b[:], ident[:]).then_inc(s_bo, 1)
            scales(0, 4)
            dve.wait_ge(s_bo, 2)
            nc.vector.tensor_tensor(beff[:], bank_a[:, 0:1], bias[:, 4:5], ALU.add).then_inc(s_beff, 1)
            done = [0]

            def then(ins):
                done[0] += 1
                ins.then_inc(s_rt, 1)
                dve.wait_ge(s_rt, done[0])

            def by_expert(t):
                return t[:].rearrange("p (n e) -> p n e", e=E)

            def by_expert_tile(t):
                return t[:].rearrange("p (e n) -> p e n", e=E)

            def over_experts(v):
                return v.rearrange("p (n o) -> p n o", o=1).to_broadcast([P, TT, E])

            def over_tiles(v):
                return v.rearrange("p (o e) -> p o e", o=1).to_broadcast([P, TT, E])

            def choose(n, first, end):
                def part(t):
                    return t[:, E * first:E * end].rearrange("p (n e) -> p n e", e=E)

                def spread(v):
                    return v[:, first:end].rearrange("p (n o) -> p n o", o=1).to_broadcast([P, end - first, E])

                number = cnt[:, 0:E].rearrange("p (o e) -> p o e", o=1).to_broadcast([P, end - first, E])
                k = 0 if n < 6 else 1
                logits, oh = ((LG, OH0), (PA, OH1))[k]
                if n in (0, 6):
                    then(nc.vector.tensor_reduce(m1[:, k, first:end], part(logits), AX.X, ALU.max))
                if n in (1, 7):
                    then(nc.vector.tensor_tensor(part(GE), part(logits), spread(m1[:, k]), ALU.is_ge))
                if n in (2, 8):
                    then(nc.vector.tensor_tensor(part(PB), part(GE), number, ALU.mult))
                if n in (3, 9):
                    then(nc.vector.tensor_reduce(ix[:, k, first:end], part(PB), AX.X, ALU.min))
                if n in (4, 10):
                    then(nc.vector.tensor_tensor(part(oh), number, spread(ix[:, k]), ALU.is_equal))
                if n == 5:
                    then(nc.vector.scalar_tensor_tensor(part(PA), part(OH0), -3e38, part(LG), ALU.mult, ALU.add))
                if n == 11:
                    nc.vector.tensor_tensor(part(MM), part(OH0), part(OH1), ALU.add).then_inc(s_mm, 1)

            rest_of_pairs = {-6: (4, 6), -5: (6, 14), -4: (14, 23), -3: (23, NP)}

            def step(at):
                for k in range(H):
                    if at.r % 2 == 1 and at.has(-3) and k == 3:
                        wait(dve, s_x2, at.pairs(-3, add=1))
                    if at.r % 2 == 1 and at.has(-3) and k == 4:
                        wait(dve, s_st2, at.pairs(-3, add=1))
                    if at.has(2):
                        c = at.mod(2)
                        wait(dve, s_S, at.value(8, 16 + k + 1))
                        if k == 0:
                            wait(dve, s_msp, at.value(1, 1))
                        nc.vector.tensor_reduce(M[:, c, 2 * k:2 * k + 2],
                                                bank_s[S_BANK[c][k]][:].rearrange("p (a s) -> p a s", a=2),
                                                AX.X, ALU.max).then_inc(s_red, 1)
                    if k == 0 and at.has(1):
                        c = at.mod(2, 1)
                        wait(dve, s_red, at.value(8, 16))
                        wait(dve, s_TM, at.value(1, 0))
                        nc.vector.tensor_copy(Mb[:, c, 0, :], M[:, c, :]).then_inc(s_hi, 1)
                        wait(dve, s_hi, at.value(1, 2))
                        nc.vector.tensor_tensor(Mb[:, c, 1, :], M[:, c, :], Mb[:, c, 0, :],
                                                ALU.subtract).then_inc(s_msp, 1)
                    if k == 2 and at.r % 2 == 1 and at.has(-3):
                        pair = at.pair(-3)
                        xp = X[:, bass.ds(pair, 1), :].rearrange("p a t -> p (a t)")
                        wait(dve, s_WO, at.pairs(-3, add=1))
                        nc.vector.scalar_tensor_tensor(xp, bank_b[:, 0:T], beff[:, 0:1], xp,
                                                       ALU.add, ALU.add).then_inc(s_x2, 1)
                    if k == 3 and at.r % 2 == 1 and at.has(-3):
                        nc.vector.bn_stats(st2[:], X[:, bass.ds(at.pair(-3), 1), :]
                                           .rearrange("p a t -> p (a t)")).then_inc(s_st2, 1)
                    if k == 4 and at.r % 2 == 1 and at.has(-3):
                        nc.vector.bn_aggr(mv2[:, at.odd_pair(-3), :], st2[:]).then_inc(s_mv2, 1)
                    if k < 3 and at.r % 2 == 0 and at.has(-4):
                        v = vv[:, at.odd_pair(-4)]
                        if k == 0:
                            wait(dve, s_mv2, at.pairs(-4, add=1))
                            nc.vector.tensor_scalar(v[:, 0:1], mv2[:, at.odd_pair(-4), 1:2], EPS, None,
                                                    ALU.add).then_inc(s_vv, 1)
                        if k == 1:
                            wait(dve, s_vv, at.pairs(-4, add=1))
                            nc.vector.tensor_scalar(v[:, 1:2], v[:, 0:1], 0.5, None, ALU.mult)
                            nc.vector.tensor_scalar(v[:, 2:3].bitcast(I32), v[:, 0:1].bitcast(I32), 1, None,
                                                    ALU.logical_shift_right).then_inc(s_sh2, 1)
                        if k == 2:
                            wait(dve, s_sh2, at.pairs(-4, add=1))
                            nc.vector.tensor_scalar(v[:, 3:4].bitcast(I32), v[:, 2:3].bitcast(I32), -1.0,
                                                    float(0x5F3759DF), ALU.mult, ALU.add).then_inc(s_guess, 1)
                    if k == 2 and at.i is None and at.r == 68:
                        for n in range(3, 12):
                            choose(n, 0, EARLY)
                    if k == 2 and at.r % 2 == 0 and at.has(-6):
                        if at.i is None and at.r == 6:
                            dve.wait_ge(s_wr, 32)
                        wait(dve, s_lg, at.pairs(-6, add=1))
                        apart(dve)
                        nc.vector.tensor_tensor(LG[:, bass.ds(E * at.pair(-6), E)], bank_b[:, 0:E],
                                                br[:], ALU.add).then_inc(s_lge, 1)
                    if k == 4 and at.has(6):
                        h = at.mod(2)
                        wait(dve, s_proj, at.value(1, 7))
                        wait(dve, s_p1, at.value(1, 5))
                        nc.vector.scalar_tensor_tensor(rc[:, h, :], bank_b[:, 0:T], bias[:, 2 * h:2 * h + 1],
                                                       tab[:, 0, :], ALU.add, ALU.mult)
                        nc.vector.scalar_tensor_tensor(rs[:, h, :], bank_b[:, T:2 * T], bias[:, 2 * h + 1:2 * h + 2],
                                                       tab[:, 1, :], ALU.add, ALU.mult).then_inc(s_rope, 1)
                    if k == 5 and at.has(-1):
                        o = bank_a[:].rearrange("p (g e) -> p g e", e=32)
                        wait(dve, s_T1, at.value(1, 0))
                        wait(dve, s_On, at.value(1, -1))
                        nc.vector.reciprocal(rden[:], o[:, :, D]).then_inc(s_rc, 1)
                        wait(dve, s_rc, at.value(1, 0))
                        half = at.mod(2, -1)
                        if half == 0:
                            wait(dve, s_BT, at.pairs(-1, add=-1))
                        nc.vector.tensor_tensor(
                            On[at.odd_pair(-1)][:, :, C * half:C * half + C].rearrange("p a (h e) -> p a h e", e=D),
                            o[:, :, 0:D].rearrange("p (a h) e -> p a h e", a=2),
                            rden[:].rearrange("p (a h o) -> p a h o", a=2, o=1).to_broadcast([P, 2, H, D]),
                            ALU.mult).then_inc(s_On, 1)
                if at.i is None and at.r == 65:
                    dve.wait_ge(s_wx, 16 * 16)
                    dve.wait_ge(s_PV, 2 * NB)
                    dve.wait_ge(s_BT, NP)
                    dve.wait_ge(s_lge, EARLY)
                    for n in range(3):
                        choose(n, 0, EARLY)
                if at.i is None and at.r in rest_of_pairs:
                    stats(*rest_of_pairs[at.r])
                if at.i is None and at.r == 0:
                    scales(4, NP)

            steps(dve, step)

            dve.wait_ge(s_wx, 16 * 16)
            dve.wait_ge(s_lge, TT)
            for n in range(12):
                choose(n, EARLY, TT)
            nc.vector.memset(by_expert_tile(PA)[:, :, 0:1], 0.0)
            then(nc.vector.memset(fresh[:], 1.0))
            then(nc.vector.memset(by_expert_tile(fresh)[:, :, 0:1], 0.0))
            nc.vector.tensor_tensor(prob[:, 1, :], m1[:, 1, :], m1[:, 0, :], ALU.subtract)
            nc.vector.tensor_tensor(by_expert(PB), by_expert(LG), over_experts(m1[:, 0, :]), ALU.subtract).then_inc(s_ex, 1)
            dve.wait_ge(s_pos, 1)
            then(nc.vector.tensor_copy(by_expert_tile(PA)[:, :, 1:TT],
                                       all_bank[:, 0:(TT - 1) * E].rearrange("p (n e) -> p e n", e=E)))
            then(nc.vector.tensor_tensor_scan(GE[:], fresh[:], PA[:], 0.0, ALU.mult, ALU.add))
            a, b = by_expert_tile(GE), PA
            then(nc.vector.tensor_tensor(nt[:, 0, :], a[:, :, TT - 1], all_bank[:, (TT - 1) * E:TT * E], ALU.add))
            then(nc.vector.tensor_tensor(b[:].rearrange("p (e n) -> p e n", e=E),
                                         nt[:, 0, :].rearrange("p (e o) -> p e o", o=1).to_broadcast([P, E, TT]),
                                         cnt[:, E:E + TT].rearrange("p (o n) -> p o n", o=1).to_broadcast([P, E, TT]),
                                         ALU.is_gt))
            then(nc.vector.tensor_reduce(nt[:, 1, :], b[:].rearrange("p (e n) -> p e n", e=E), AX.X, ALU.add))
            upto = cnt[:, E + TT + NS:].rearrange("p (e f) -> p e f", e=E)
            then(nc.vector.tensor_tensor(b[:, 0:E * E].rearrange("p (e f) -> p e f", e=E), upto,
                                         nt[:, 1, :].rearrange("p (o f) -> p o f", o=1).to_broadcast([P, E, E]), ALU.mult))
            then(nc.vector.tensor_reduce(nt[:, 2, :], b[:, 0:E * E].rearrange("p (e f) -> p e f", e=E), AX.X, ALU.add))
            then(nc.vector.tensor_tensor(nt[:, 3, :], nt[:, 2, :], nt[:, 1, :], ALU.subtract))
            a = a.rearrange("p e n -> p n e")
            then(nc.vector.tensor_tensor(a, a, by_expert(before_bank), ALU.add))
            then(nc.vector.tensor_scalar(nt[:, 3, :], nt[:, 3, :], float(P), None, ALU.mult))
            then(nc.vector.tensor_tensor(a, a, over_tiles(nt[:, 3, :]), ALU.add))
            for k, oh in enumerate((OH0, OH1)):
                then(nc.vector.tensor_tensor(by_expert(b), a, by_expert(oh), ALU.mult))
                then(nc.vector.tensor_reduce(slot_f[:, k, :], by_expert(b), AX.X, ALU.add))
                nc.vector.tensor_copy(slot[:, k, :], slot_f[:, k, :]).then_inc(s_slot, 1)
            big = xg[0:1].rearrange("p a t -> p (a t)")[:, 0:NS * E].rearrange("p (j e) -> p j e", e=E)
            then(nc.vector.tensor_tensor(big, nt[0:1, 2, :].rearrange("p (o e) -> p o e", o=1).to_broadcast([1, NS, E]),
                                         cnt[0:1, E + TT:E + TT + NS].rearrange("p (j o) -> p j o", o=1)
                                         .to_broadcast([1, NS, E]), ALU.is_le))
            then(nc.vector.tensor_reduce(owner_f[:], big, AX.X, ALU.add))
            then(nc.vector.tensor_scalar(owner_f[:], owner_f[:], float(E - 1), None, ALU.min))
            nc.vector.tensor_copy(owner[:], owner_f[:]).then_inc(s_owner, 1)
            def product(at, n, base):
                if at.has(-1, n):
                    implied(dve, at, s_h, at.value(1, base - 2))
                    wait(dve, s_si, at.value(1, base))
                    nc.vector.tensor_tensor(ar[at.mod(2, -1)][:], sg[:, at.mod(2, -1), 0:I],
                                            up_bank[at.mod(2, -1)][:, I:2 * I], ALU.mult).then_inc(s_a, 1)

            def shared(at):
                product(at, TT, 0)
                if at.has(-4, TT):
                    wait(dve, s_d, at.value(1, -3))
                    apart(dve)
                    xp = X[:, bass.ds(at.batch(-4), 1), :].rearrange("p a t -> p (a t)")
                    nc.vector.tensor_tensor(xp, xp, down_bank[at.mod(2, -4)][:, 0:T], ALU.add).then_inc(s_ye, 1)

            steps(dve, shared, 0, (6, 32), TT + 4, 2)

            def slot_products(at):
                product(at, NS, TT)
                if at.has(-1, NS):
                    wait(dve, s_put[at.mod(8, -1)], at.turns(-1, 8, 16))
                    nc.vector.tensor_copy(ids_out[:, at.mod(8, -1):at.mod(8, -1) + 1],
                                          xg[:, at.mod(8, -1), T:T + 1].bitcast(I32)).then_inc(s_idc, 1)
                if at.has(-4, NS):
                    wait(dve, s_d, at.value(1, TT - 3))
                    implied(dve, at, s_put[at.mod(8, -4)], at.turns(-4, 8, 16))
                    nc.vector.tensor_copy(ys[:, at.mod(8, -4), :], down_bank[at.mod(2)][:, 0:T]).then_inc(s_ye, 1)

            steps(dve, slot_products, 0, (16, 80), NS + 4, 8)

            dve.wait_ge(s_ex, 3)
            then(nc.vector.tensor_reduce(prob[:, 2, :], by_expert(PC), AX.X, ALU.add))
            then(nc.vector.reciprocal(prob[:, 3, :], prob[:, 2, :]))
            then(nc.vector.tensor_tensor(prob[:, 1, :], prob[:, 0, :], prob[:, 3, :], ALU.mult))
            then(nc.vector.scalar_tensor_tensor(prob[:, 2, :], prob[:, 3, :], 1e-9, prob[:, 1, :], ALU.add, ALU.add))
            then(nc.vector.reciprocal(prob[:, 0, :], prob[:, 2, :]))
            nc.vector.tensor_tensor(gate[:, 0, :], prob[:, 3, :], prob[:, 0, :], ALU.mult)
            then(nc.vector.tensor_tensor(gate[:, 1, :], prob[:, 1, :], prob[:, 0, :], ALU.mult))

            def combine(g):
                dve.wait_ge(s_y[g % 4], 32 * (g // 4 + 1))
                wait(dve, s_comb, 4 * (g - 1))
                for k in range(2):
                    if k == 1:
                        dve.wait_ge(s_hs, 4 * g + 4)
                    for n in range(4):
                        last = nc.vector.scalar_tensor_tensor(
                            (half_sum[4 * (g % 2) + n], X[:, 4 * g + n, :])[k], pair_in[:, g % 4, k, n, :],
                            gate[:, k, 4 * g + n:4 * g + n + 1], (X[:, 4 * g + n, :], half_sum[4 * (g % 2) + n])[k],
                            ALU.mult, ALU.add)
                        last.then_inc((s_hs, s_comb)[k], 1)

            for g in range(TT // 4):
                combine(g)

        @block.tensor
        def _(pe):
            pe.wait_ge(s_wd, 32)
            pe.wait_ge(s_w, 48)
            nc.tensor.matmul(bank_a[:, 0:1], w[:, 5, :], bias[:, 5:6], start=True, stop=True).then_inc(s_bo, 1)
            pe.wait_ge(s_beff, 1)

            def held(at, bank, main):
                for sem_, value, most in ((main,) if at.i is not None else (main, *readers(at, bank))):
                    wait(pe, sem_, value, most)

            def readers(at, bank):
                even = at.r % 2 == 0
                if bank is bank_a:
                    return ((s_tme, at.value(1, 1), NB), (s_On, at.value(1, -1), NB),
                            (s_Ve, at.pairs(0 if even else 1, add=1), NP))
                last, norm = (-4, -8) if even else (-3, -7)
                return ((s_rope, at.value(1, 6), NB), (s_BTe, at.pairs(last, add=1), NP),
                        (s_x2, at.pairs(-4 if even else -5, add=1), NP),
                        (s_xte, at.pairs(norm if even else -7, add=1), NP), (s_lge, at.pairs(norm, add=1), NP))

            def values(at, group, chunk):
                off = -group
                if chunk == 0:
                    wait(pe, s_exp, at.value(8, 8 * off + 4 * group + 4))
                    if group == 0:
                        wait(pe, s_Ve, at.pairs(0, add=1))
                        wait(pe, s_Oe, at.value(1, 0))
                b = at.mod(2, off)
                for j in range(4):
                    h = 4 * group + j
                    last = nc.tensor.matmul(bank_o[32 * j:32 * j + 32, T * group:T * group + T],
                                            V[at.odd_pair(off)][:, chunk, b, h, :],
                                            Pr[h][:, T * chunk:T * chunk + T],
                                            start=(chunk == 0), stop=(chunk == 1))
                if chunk == 1:
                    last.then_inc(s_PV, 1)

            def step(at):
                even = at.r % 2 == 0
                for k in range(H):
                    if at.has(2):
                        c = at.mod(4, 2)
                        if k == 0:
                            v = 32 * ((at.r + 2) // 4 + 1)
                            wait(pe, s_stk[c], v if at.i is None else 32 * at.i + v)
                        wait(pe, s_red, at.value(8, 16 + k + 1 - S_BACK[at.mod(2)][k]))
                        for t in range(2):
                            last = nc.tensor.matmul(bank_s[S_BANK[at.mod(2)][k]][:, T * t:T * t + T],
                                                    Q[c][0:KR, k, P * t:P * t + P], K[c][0:KR, k, :],
                                                    start=True, stop=True)
                        last.then_inc(s_S, 1)
                    if k == 4 and at.has(6):
                        p = at.odd_pair(6)
                        if even:
                            wait(pe, s_xn, at.pairs(6, add=1))
                            held(at, bank_b, (s_lge, at.pairs(-6, add=1), NP))
                        else:
                            wait(pe, s_ck[p], at.turns(5, 4, 16, 16))
                            held(at, bank_b, (s_x2, at.pairs(-3, add=1), NP))
                        source = xn if even else ctx_k
                        for r in range(2):
                            last = nc.tensor.matmul(bank_b[:, T * r:T * r + T], w[:, r if even else 2 + r, :],
                                                    source[:, p, :], start=True, stop=True)
                        last.then_inc(s_proj, 1)
                    if at.has(0):
                        c = at.mod(4)
                        if k == 0:
                            m = at.mod(2)
                            v = 16 * (at.r // 2 + 1)
                            wait(pe, s_mr[m], v if at.i is None else 32 * at.i + v)
                        wait(pe, s_exp, at.value(8, k - 1))
                        for s in range(2):
                            last = nc.tensor.matmul(bank_st[k % 2][:, T * s:T * s + T],
                                                    K[c][0:MROW + 2, k, P * s:P * s + P],
                                                    Q[c][0:MROW + 2, k, :], start=True, stop=True)
                        last.then_inc(s_ST, 1)
                    if not even and k == 1 and at.has(-3):
                        held(at, bank_b, (s_BTe, at.pairs(-3, add=1), NP))
                        nc.tensor.matmul(bank_b[:, 0:T], w[:, 5, :], OT[:], start=True, stop=True).then_inc(s_WO, 1)
                    if k == 2 and at.has(1):
                        wait(pe, s_msp, at.value(1, 2))
                        held(at, bank_a, (s_On, at.value(1, -1), NB) if even else (s_Ve, at.pairs(1, add=1), NP))
                        nc.tensor.transpose(bank_a[:].bitcast(BF16)[0:4 * H, 0:P],
                                            Mb[:, at.mod(2, 1)].rearrange("p a h -> p (a h)"),
                                            ident_b[:]).then_inc(s_TM, 1)
                    if k in (1, 2) and at.has(-1):
                        values(at, 1, k - 1)
                    if even and k == 1 and at.has(-6):
                        if at.i is None and at.r == 6:
                            pe.wait_ge(s_wr, 32)
                        held(at, bank_b, (s_xte, at.pairs(-6, add=1), NP))
                        for c in range(2):
                            last = nc.tensor.matmul(bank_b[:, 0:E], xTs[0][:, c, :], wr[:, c, :],
                                                    start=(c == 0), stop=(c == 1))
                        last.then_inc(s_lg, 1)
                    if k == 4 and at.has(-1):
                        wait(pe, s_Oe, at.value(1, 0))
                        held(at, bank_a, (s_tme, at.value(1, 2), NB))
                        for t in range(2):
                            for g in range(2):
                                col = P * (2 * t + g)
                                last = nc.tensor.transpose(bank_a[:, col:col + P],
                                                           O[:, T * g + P * t:T * g + P * t + P], ident[:])
                        last.then_inc(s_T1, 1)
                    if k in (5, 6) and at.has(0):
                        values(at, 0, k - 5)
                    if even and k == 6 and at.has(-2):
                        wait(pe, s_On, at.value(1, 0))
                        held(at, bank_b, (s_rope, at.value(1, 7), NB))
                        if at.i is None:
                            wait(pe, s_lge, at.pairs(-6, add=1))
                        for t in range(2):
                            last = nc.tensor.transpose(bank_b[:, P * t:P * t + P], On[at.odd_pair(-2)][:, t, :], ident[:])
                        last.then_inc(s_BT, 1)
                    if even and k == 7 and at.has(2):
                        p = at.odd_pair(2)
                        wait(pe, s_cv[p], at.turns(2, 4, 16, 16))
                        held(at, bank_a, (s_On, at.value(1, 0), NB))
                        if at.i is None:
                            wait(pe, s_tme, at.value(1, 2))
                        for s in range(2):
                            last = nc.tensor.matmul(bank_a[:, P * s:P * s + P], ctx_v[:, p, P * s:P * s + P],
                                                    w[:, 4, :], start=True, stop=True)
                        last.then_inc(s_vp, 1)
                    if not even and k == 7 and at.has(-5):
                        wait(pe, s_xs, at.pairs(-5, add=1))
                        held(at, bank_b, (s_rope, at.value(1, 7), NB))
                        if at.i is None:
                            wait(pe, s_x2, at.pairs(-3, add=1), NP)
                        for c in range(2):
                            last = nc.tensor.transpose(bank_b[:, P * c:P * c + P], xs[:, P * c:P * c + P], ident[:])
                        last.then_inc(s_xt, 1)

            pe.wait_ge(s_bo, 2)
            pe.wait_ge(s_zero, 7)
            steps(pe, step)

            pe.wait_ge(s_lge, NP)
            pe.wait_ge(s_x2, NP)
            pe.wait_ge(s_On, NB)
            pe.wait_ge(s_BTe, NP)
            pe.wait_ge(s_red, H * NB)
            pe.wait_ge(s_exp, H * NB)
            pe.wait_ge(s_Oe, NB)
            pe.wait_ge(s_wx, 16 * 16)

            for n, (first, end) in enumerate(((0, EARLY), (EARLY, TT))):
                pe.wait_ge(s_mm, n + 1)
                for bank, which in ((before_bank, 0), (all_bank, 1)):
                    last = nc.tensor.matmul(bank[:, E * first:E * end], low[:, which, :], MM[:, E * first:E * end],
                                            start=True, stop=True)
            last.then_inc(s_pos, 1)

            def tile(at, n, base, load, gate_up, down):
                if at.has(0, n):
                    rows_ = load(at)
                    if at.has(-1, n):
                        wait(pe, s_te, at.value(1, base))
                    for c in range(2):
                        last = nc.tensor.transpose(tile_bank[at.mod(2)][:, P * c:P * c + P],
                                                   rows_[:, P * c:P * c + P], ident[:])
                    last.then_inc(s_t, 1)
                if at.has(-1, n):
                    m = at.mod(2, -1)
                    implied(pe, at, s_te, at.value(1, base))
                    weights = gate_up(at)
                    for c in range(2):
                        last = nc.tensor.matmul(up_bank[m][:, 0:2 * I], xTs[m][:, c, :], weights(c),
                                                start=(c == 0), stop=(c == 1))
                    last.then_inc(s_g, 1)
                if at.has(-2, n):
                    m = at.mod(2, -2)
                    implied(pe, at, s_he, at.value(1, base - 3))
                    wait(pe, s_a, at.value(1, base - 1))
                    nc.tensor.transpose(mid_bank[m][:, 0:P], ar[m][:], ident[:]).then_inc(s_h, 1)
                if at.has(-4, n):
                    m = at.mod(2, -4)
                    implied(pe, at, s_ye, at.value(1, base - 5))
                    implied(pe, at, s_he, at.value(1, base - 3))
                    weights = down(at)
                    nc.tensor.matmul(down_bank[m][:, 0:T], aT[m][:, 0:P], weights,
                                     start=True, stop=True).then_inc(s_d, 1)

            pe.wait_ge(s_slot, 2)

            def row_copy(at):
                wait(pe, s_in, at.value(1, 1))
                return xn[:, at.mod(2), :]

            steps(pe, lambda at: tile(at, TT, 0, row_copy, lambda at: lambda c: sgu[:, c, :], lambda at: sd[:]),
                  0, (6, 32), TT + 4, 2)

            pe.wait_ge(s_owner, 1)
            expert = {}

            def slot_rows(at):
                wait(pe, s_xg[at.mod(8)], at.turns(0, 8, 16, 16))
                return xg[:, at.mod(8), :]

            def slot_gate_up(at):
                e = expert_of(at, -1)
                if at.i is None:
                    apart(pe)
                return lambda c: wgu[:, bass.ds(e, 1), c, :].rearrange("p a i -> p (a i)")

            def slot_down(at):
                key = (at.i is None, at.r - 4)
                e = expert[key] if key in expert else expert_of(at, -4)
                if at.i is None:
                    apart(pe)
                return wd[:, bass.ds(e, 1), :].rearrange("p a t -> p (a t)")

            def expert_of(at, off):
                e = nc.values_load(owner[0:1, bass.ds(at.batch(off), 1)], engines=[mybir.EngineType.PE],
                                   min_val=0, max_val=E - 1,
                                   skip_runtime_bounds_check_because="a count of experts, at most E - 1 by its minimum")
                expert[(at.i is None, at.r + off)] = e
                return e

            steps(pe, lambda at: tile(at, NS, TT, slot_rows, slot_gate_up, slot_down), 0, (8, 80), NS + 4, 8)


def kernel(**inputs):
    import numpy as np
    import concourse.bacc as bacc
    from concourse.bass_utils import run_bass_kernel_spmd as run

    H, D, T = 8, 8, 256
    x = np.ascontiguousarray(np.asarray(inputs["x"]).reshape(4096, T))
    ctx = np.ascontiguousarray(np.asarray(inputs["ctx_2048"]).reshape(4096, T))

    def by_channel(a, turn=0):
        v = np.asarray(a).reshape(H, D, *np.asarray(a).shape[1:])
        return np.roll(v, -turn, axis=1).swapaxes(0, 1).reshape(np.asarray(a).shape)

    g = {n: np.asarray(inputs["L0_xattn_" + n]) for n in ("Wq", "Wk", "Wv", "Wo", "bq", "bk", "bv", "bo")}
    w6 = np.stack([by_channel(g["Wq"]).T, by_channel(g["Wq"], 4).T, by_channel(g["Wk"]).T,
                   by_channel(g["Wk"], 4).T, g["Wv"].T, g["Wo"].T], axis=1)
    b6 = np.stack([by_channel(g["bq"]), by_channel(g["bq"], 4), by_channel(g["bk"]), by_channel(g["bk"], 4),
                   g["bo"], g["bv"]], axis=1)
    freq = (1.0 / np.float32(10000.0) ** (np.arange(0, D, 2, dtype=np.float32) / np.float32(D))).astype(np.float32)
    ang = np.arange(T, dtype=np.float32)[None, :] * np.tile(freq, 2)[:, None]
    sign = np.where(np.arange(D) < D // 2, -1.0, 1.0).astype(np.float32)[:, None]
    one = np.stack([np.cos(ang), np.sin(ang) * sign], axis=1).astype(np.float32)
    rope = np.tile(np.repeat(one, H, axis=0), (2, 1, 1))

    arrays = {"x_dram": x, "ctx_dram": ctx, "w6": np.ascontiguousarray(w6),
              "bias6": np.ascontiguousarray(np.tile(b6, (2, 1))), "rope": np.ascontiguousarray(rope),
              "ident_dram": np.eye(128, dtype=np.float32)}
    m = {n: np.asarray(inputs["L0_ffn_" + n]) for n in ("Wr", "bias", "Wg", "Wu", "Wd", "sWg", "sWu", "sWd")}
    E, P = 16, 128
    counts = np.concatenate([np.arange(E) - 1024.0, np.arange(32) * 128.0, np.arange(80),
                             np.tril(np.ones((E, E))).reshape(-1)]).astype(np.float32)
    below = np.stack([np.triu(np.ones((P, P)), 1), np.ones((P, P))], axis=1).astype(np.float32)
    arrays |= {
        "w_router": np.ascontiguousarray(m["Wr"].T), "b_router": np.tile(m["bias"][None], (P, 1)),
        "w_gu": np.concatenate([m["Wg"], m["Wu"]], axis=2), "w_down": np.ascontiguousarray(m["Wd"]),
        "s_gu": np.concatenate([m["sWg"], m["sWu"]], axis=1), "s_down": np.ascontiguousarray(m["sWd"]),
        "counts": np.tile(counts, (P, 1)), "below": below,
    }
    nc = bacc.Bacc("TRN2", target_bir_lowering=False, num_devices=1)
    args = [nc.dram_tensor(n, a.shape, mybir.dt.from_np(a.dtype), kind="ExternalInput").ap() for n, a in arrays.items()]
    out = nc.dram_tensor("out", (4096, T), F32, kind="ExternalOutput").ap()
    xattn_moe(nc, *args, out)
    r = run(nc, [arrays], core_ids=[0])
    return r.results[0]["out"].reshape(64, 64, T)
```
